# Optimizing a Trainium2 kernel written in Bass

```python
import numpy as np
import jax
import jax.numpy as jnp

def _softmax(x, axis=-1):
    return jax.nn.softmax(x, axis=axis)

def _gelu(x):
    return jax.nn.gelu(x, approximate=True)

def _silu(x):
    return jax.nn.silu(x)

def _sigmoid(x):
    return jax.nn.sigmoid(x)

def _layernorm(x, axis=-1, eps=1e-05):
    m = jnp.mean(x, axis=axis, keepdims=True)
    v = jnp.var(x, axis=axis, keepdims=True)
    return (x - m) / jnp.sqrt(v + eps)

def _scatter_add(tgt, idx, src, axis=0):
    return tgt.at[idx].add(src)

def _segment_sum(src, seg, n):
    return jax.ops.segment_sum(src, seg, n)
kernel_name = 'mk_flamingo_gated_d1_seqx_r4_8c2ff1'

def setup_inputs(seed: int=0):
    np.random.seed(seed)
    _w = jnp.asarray

    def _rec_inputs():
        import jax
        import jax.numpy as jnp
        _rk = jax.random.key(seed)
        x = -0.000125 + 0.9999 * jax.random.normal(jax.random.fold_in(_rk, 1), (4, 512, 512), jnp.float32)
        _lenS = 512 - jax.random.randint(jax.random.fold_in(_rk, 7), (4,), 0, max(1, 512 // 4) + 1, jnp.int32)
        _lenS2 = 512 - jax.random.randint(jax.random.fold_in(_rk, 8), (4,), 0, max(1, 512 // 4) + 1, jnp.int32)
        itok_BxS_13_99985 = jax.random.randint(jax.random.fold_in(_rk, 11), (4, 512), 13, 99986, jnp.int32)
        _ctx_2048P = jax.random.normal(jax.random.fold_in(_rk, 12), (4, 16, 512), jnp.float32)
        _ctx_2048c = jax.random.dirichlet(jax.random.fold_in(_rk, 512), 0.3 * jnp.ones((16,), jnp.float32), (4, 512))
        _ctx_2048t = jnp.einsum('bsk,bkd->bsd', _ctx_2048c, _ctx_2048P)
        _ctx_2048t = _ctx_2048t * jax.lax.rsqrt(jnp.mean(jnp.square(_ctx_2048t)) + 1e-12) * 0.953939
        ctx_2048 = 6.82029e-06 + 0.0200006 * (_ctx_2048t + 0.3 * jax.random.normal(jax.random.fold_in(_rk, 612), (4, 512, 512), jnp.float32))
        _g = jax.random.normal(jax.random.fold_in(_rk, 9001), (2, 1), jnp.float32)
        _g = jnp.sign(_g) * jnp.maximum(jnp.abs(_g), 1.0) + (_g == 0) * 1.0
        g_xattn = _g[0]
        g_ffn = _g[1]
        return (x, itok_BxS_13_99985, ctx_2048, g_xattn, g_ffn)
    x, itok_BxS_13_99985, ctx_2048, g_xattn, g_ffn = _rec_inputs()

    def _L0_xattn_setup():
        import jax, jax.numpy as jnp
        import numpy as np
        B, S, D = (4, 1024, 512)
        E = 4
        F = 2048 // E
        VOCAB = 25000
        key = jax.random.key(seed)
        k1, k2, k3, k4, k5 = jax.random.split(key, 5)
        hidden_states = jax.random.normal(k1, (B, S, D), dtype=jnp.float32)
        token_ids = jax.random.randint(k2, (B, S), 0, VOCAB, dtype=jnp.int64)
        Wg = jax.random.normal(k3, (E, F, D), dtype=jnp.float32) * 0.02
        Wu = jax.random.normal(k4, (E, F, D), dtype=jnp.float32) * 0.02
        Wd = jax.random.normal(k5, (E, D, F), dtype=jnp.float32) * 0.02
        return {'hidden_states': hidden_states, 'token_ids': token_ids, 'Wg': Wg, 'Wu': Wu, 'Wd': Wd}
    _L0_xattn_all = _L0_xattn_setup()
    _L0_xattn_in = {k: v for k, v in _L0_xattn_all.items() if k in ()}
    del _L0_xattn_all

    def _L0_ffn_setup():
        import jax, jax.numpy as jnp
        import numpy as np
        E4M3_MAX = 448.0

        def _quant_e4m3(t):
            amax = jnp.max(jnp.abs(t)).astype(jnp.float32)
            scale = jnp.maximum(amax / E4M3_MAX, 1e-12)
            fp8 = (t.astype(jnp.float32) / scale).astype(jnp.float8_e4m3fn)
            return (fp8, scale)

        def _scaled_mm(a_fp8, b_fp8, sa, sb):
            acc = jnp.matmul(a_fp8.astype(jnp.float32), b_fp8.astype(jnp.float32))
            return (acc * (sa * sb)).astype(jnp.bfloat16)
        key = jax.random.key(seed)
        k1, k2 = jax.random.split(key)
        x = jax.random.normal(k1, (4, 512, 512), dtype=jnp.bfloat16)
        weight = (jax.random.normal(k2, (512, 512), dtype=jnp.bfloat16) * 0.02).astype(jnp.bfloat16)
        return {'x': x, 'weight': weight}
    _L0_ffn_all = _L0_ffn_setup()
    _L0_ffn_in = {k: v for k, v in _L0_ffn_all.items() if k in ('weight',)}
    del _L0_ffn_all
    return {'x': x, 'itok_BxS_13_99985': itok_BxS_13_99985, 'ctx_2048': ctx_2048, 'g_xattn': g_xattn, 'g_ffn': g_ffn, 'L0_ffn_weight': _L0_ffn_in['weight']}

def reference(x, itok_BxS_13_99985, ctx_2048, g_xattn, g_ffn, L0_ffn_weight):
    import jax
    import jax.numpy as jnp

    def _L0_xattn_ref(hidden_states, token_ids, Wg, Wu, Wd):
        import jax, jax.numpy as jnp
        import numpy as np
        B, S, D = (4, 1024, 512)
        E = 4
        F = 2048 // E
        VOCAB = 25000
        tokens_per_expert = VOCAB // E
        tid = jnp.clip(token_ids, 0, VOCAB - 1)
        expert_ids = jnp.minimum(tid // tokens_per_expert, E - 1)
        out = jnp.zeros_like(hidden_states)
        for e in range(E):
            g = jax.nn.silu(jnp.einsum('bsd,fd->bsf', hidden_states, Wg[e]))
            u = jnp.einsum('bsd,fd->bsf', hidden_states, Wu[e])
            y = jnp.einsum('bsf,df->bsd', g * u, Wd[e])
            out = jnp.where((expert_ids == e)[..., None], y, out)
        return out

    def _L0_ffn_ref(x, weight):
        import jax, jax.numpy as jnp
        import numpy as np
        E4M3_MAX = 448.0

        def _quant_e4m3(t):
            amax = jnp.max(jnp.abs(t)).astype(jnp.float32)
            scale = jnp.maximum(amax / E4M3_MAX, 1e-12)
            fp8 = (t.astype(jnp.float32) / scale).astype(jnp.float8_e4m3fn)
            return (fp8, scale)

        def _scaled_mm(a_fp8, b_fp8, sa, sb):
            acc = jnp.matmul(a_fp8.astype(jnp.float32), b_fp8.astype(jnp.float32))
            return (acc * (sa * sb)).astype(jnp.bfloat16)
        w_fp8, w_scale = _quant_e4m3(weight)
        x2d = x.reshape(-1, x.shape[-1])
        x_fp8, x_scale = _quant_e4m3(x2d)
        out2d = _scaled_mm(x_fp8, w_fp8.T, x_scale, w_scale)
        return out2d.reshape(*x.shape[:-1], out2d.shape[-1])
    x = x + jnp.tanh(g_xattn[0]) * _L0_xattn_ref(_layernorm(x, axis=-1), itok_BxS_13_99985, ctx_2048, ctx_2048, ctx_2048)
    x = x + jnp.tanh(g_ffn[0]) * _L0_ffn_ref(_layernorm(x, axis=-1), L0_ffn_weight)
    return x

_drawn_inputs = setup_inputs


def setup_inputs(seed=0):
    import zlib

    import numpy as np

    out = dict(_drawn_inputs(seed))
    spreads = {}
    factors = {}
    for name, (base, spread) in spreads.items():
        noise = np.random.default_rng([zlib.crc32(name.encode()), seed]).standard_normal(out[name].shape)
        drawn = base * np.exp(spread * noise) if base else spread * noise
        out[name] = jnp.asarray(drawn.astype(out[name].dtype))
    for name, factor in factors.items():
        out[name] = (out[name] * factor).astype(out[name].dtype)
    return out
```

```python
from contextlib import ExitStack

import concourse.bass as bass
from concourse import mybir

ALU = mybir.AluOpType
ACT = mybir.ActivationFunctionType
AX = mybir.AxisListType
F32 = mybir.dt.float32
F16 = mybir.dt.float16
BF16 = mybir.dt.bfloat16
I32 = mybir.dt.int32
I16 = mybir.dt.int16

P = 128
VOCAB = 25000
EPS = 1e-5
H_SHIFT = 10
EXP_MASK = 0x7F800000
ONE = 1 << 23
BIAS = 127
W_EXP = 38
E4M3_MAX = 448.0


def gated_experts_kernel(nc, x, ids, ctx_t, g_x, g_f, wf_t, out):
    T, D = x.shape
    E = ctx_t.shape[0]
    K = D // P
    TILES = T // P
    JOBS = TILES + E - 1
    C = ids.shape[1]
    PER = VOCAB // E
    assert ids.shape == (P, C) and P * C == T and D * 4 == 2048

    with ExitStack() as stack:
        def sb(name, shape, dt):
            return stack.enter_context(nc.sbuf_tensor(name, shape, dt))

        def psum(name, shape, dt):
            return stack.enter_context(nc.psum_tensor(name, shape, dt))

        def sem(name):
            return stack.enter_context(nc.semaphore(name))

        ident = sb("ident", [P, P], F32)
        ident_bf = sb("ident_bf", [P, P], BF16)
        below = sb("below", [P, P], F16)
        above = sb("above", [P, P], F16)
        ones_h = sb("ones_h", [P, P], F16)
        ones_r = sb("ones_r", [2, P], F32)
        iota_q = sb("iota_q", [P, P], F16)
        iota_tile = sb("iota_tile", [P, C, TILES], F32)
        token_no = sb("token_no", [P, C], F32)
        iota_job = sb("iota_job", [P, JOBS], F32)
        iota_slot = sb("iota_slot", [P, JOBS], F32)
        minus_half = sb("minus_half", [P, 1], F32)
        ids_s = sb("ids_s", [P, C], I32)
        reach = sb("reach", [P, E + 1, C], F32)
        member = sb("member", [P, E, C], F32)
        scan_one = sb("scan_one", [P, E * C], F32)
        count = sb("count", [P, E * C], F32)
        row_cum = sb("row_cum", [P, E + 1], F16)
        place = sb("place", [P, E, C], F32)
        slot_f = sb("slot_f", [P, C], F32)
        slot_i = sb("slot_i", [P, C], I32)
        q_i = sb("q_i", [P, C], I32)
        q_f = sb("q_f", [P, C], F32)
        tile_i = sb("tile_i", [P, C], I32)
        tile_f = sb("tile_f", [P, C], F32)
        hit = sb("hit", [P, C, TILES], F32)
        pick = sb("pick", [P, C, TILES], F16)
        onehot = sb("onehot", [P, C, P], F16)
        token_of = sb("token_of", [P, TILES], I32)
        start = sb("start", [P, E], F32)
        start_i = sb("start_i", [P, E], I32)
        bound = sb("bound", [P, E], F32)
        job_e = sb("job_e", [P, JOBS], F32)
        job_slot = sb("job_slot", [P, JOBS], F32)
        slot_e = sb("slot_e", [P, JOBS], F32)
        mask = sb("mask", [P, JOBS], F32)
        job_expert_i = sb("job_expert_i", [1, JOBS], I32)
        job_tile_i = sb("job_tile_i", [1, JOBS], I32)
        g_s = sb("g_s", [P, 2], F32)
        tg = sb("tg", [P, 2], F32)
        wmax_e = sb("wmax_e", [P, E], F32)
        wmax = sb("wmax", [P, 2], F32)
        wmax_g = sb("wmax_g", [2, 1], F32)
        wmax_d = sb("wmax_d", [2, 2], F32)
        wmax_b = sb("wmax_b", [P, 2], F32)
        wexp = sb("wexp", [P, 1], I32)
        s_w = sb("s_w", [P, 1], I32)
        inv_a = sb("inv_a", [P, 1], I32)
        z_mul = sb("z_mul", [P, 1], I32)
        inv_y = sb("inv_y", [P, 1], I32)
        y_mul = sb("y_mul", [P, 1], F32)
        job_mul = sb("job_mul", [P, JOBS], F32)
        wf_scale = sb("wf_scale", [P, 1], F32)
        wf_inv = sb("wf_inv", [P, 1], F32)
        rmax = sb("rmax", [P, TILES], F32)
        xmax = sb("xmax", [P, 1], F32)
        xmax_g = sb("xmax_g", [1, 1], F32)
        x_scale = sb("x_scale", [P, 1], F32)
        x_inv = sb("x_inv", [P, 1], F32)
        out_scale = sb("out_scale", [P, 1], F32)
        x1 = sb("x1", [P, TILES * D], F32)
        w32 = sb("w32", [P, E * K * D], F32)
        h2 = w32
        w_hi = sb("w_hi", [P, E * K * D], F16)
        w_lo = sb("w_lo", [P, E * K * D], F16)
        hT_hi = sb("hT_hi", [P, TILES * D], F16)
        hT_lo = sb("hT_lo", [P, TILES * D], F16)
        h = sb("h", [P, D], F32)
        sg = sb("sg", [P, D], F32)
        z = sb("z", [P, D], F32)
        zT_hi = sb("zT_hi", [P, D], F16)
        zT_lo = sb("zT_lo", [P, D], F16)
        bn1 = sb("bn1", [P, 6], F32)
        mv1 = sb("mv1", [P, 2], F32)
        var1 = sb("var1", [P, 1], F32)
        rstd1 = sb("rstd1", [P, 1], F32)
        bn2 = sb("bn2", [P, 6], F32)
        mv2 = sb("mv2", [P, 2], F32)
        var2 = sb("var2", [P, 1], F32)
        rstd2 = sb("rstd2", [P, 1], F32)
        wf = sb("wf", [P, K * D], BF16)
        wf_v = sb("wf_v", [P, K * D], F32)
        wf_e = sb("wf_e", [P, K * D], BF16)
        wf_m = sb("wf_m", [P, K * D], BF16)
        wf_q = sb("wf_q", [P, K * D], BF16)
        v = sb("v", [P, 2, D], F32)
        ve = sb("ve", [P, 2, D], BF16)
        vm = sb("vm", [P, 2, D], BF16)
        vt = sb("vt", [P, 2, D], F32)
        q8 = sb("q8", [P, 2, D], BF16)
        qT = sb("qT", [P, 2, D], BF16)
        y8 = sb("y8", [P, 2, D], BF16)

        a_ps = psum("a_ps", [P, D], F32)
        y_ps = psum("y_ps", [P, D], F32)
        hT_ps = psum("hT_ps", [P, D], F32)
        zT_ps = psum("zT_ps", [P, D], F32)
        r_ps = psum("r_ps", [P, 512], F32)
        c_ps = psum("c_ps", [P, 512], F32)
        qT_ps = [psum(f"qT_ps{i}", [P, 2 * D], BF16) for i in range(2)]
        f_ps = [a_ps, y_ps]
        base_ps = r_ps[:, 0:E]
        start_ps = c_ps[:, 64:64 + E + 1]
        sort_ps = c_ps[:, 0:TILES]

        ids_loaded, g_loaded, wf_loaded = sem("ids_loaded"), sem("g_loaded"), sem("wf_loaded")
        w_loaded = [sem(f"w_loaded{e}") for e in range(E)]
        x_gathered = [sem(f"x_gathered{i}") for i in range(TILES)]
        stored = sem("stored")
        pool_const, pool_fill = sem("pool_const"), sem("pool_fill")
        route = sem("route")
        sums_done, sort_done = sem("sums_done"), sem("sort_done")
        onehot_done = sem("onehot_done")
        tokens_ready, jobs_ready = sem("tokens_ready"), sem("jobs_ready")
        tanh_done = sem("tanh_done")
        wm_step, wmax_T, wmax_B = sem("wm_step"), sem("wmax_T"), sem("wmax_B")
        w_scales = sem("w_scales")
        w_hi_done, w_lo_done = sem("w_hi_done"), sem("w_lo_done")
        bn1_done, mv1_done, var1_done, rstd1_done = sem("bn1_done"), sem("mv1_done"), sem("var1_done"), sem("rstd1_done")
        bn2_done, mv2_done, var2_done, rstd2_done = sem("bn2_done"), sem("mv2_done"), sem("var2_done"), sem("rstd2_done")
        h_done, hT_done = sem("h_done"), sem("hT_done")
        hT_hi_done, hT_lo_done = sem("hT_hi_done"), sem("hT_lo_done")
        a_done, silu_done, z_done, zT_done = sem("a_done"), sem("silu_done"), sem("z_done"), sem("zT_done")
        zT_hi_done, zT_lo_done, y_done, x1_done = sem("zT_hi_done"), sem("zT_lo_done"), sem("y_done"), sem("x1_done")
        h2_done, rmax_done = sem("h2_done"), sem("rmax_done")
        wfv_done, wfe_done, wfm_done, wft_done, wfq_done = (sem("wfv_done"), sem("wfe_done"), sem("wfm_done"),
                                                            sem("wft_done"), sem("wfq_done"))
        xm_step, xmax_T, xmax_B = sem("xm_step"), sem("xmax_T"), sem("xmax_B")
        v_done, ve_done, vm_done, vt_done, q8_done = (sem("v_done"), sem("ve_done"), sem("vm_done"), sem("vt_done"),
                                                      sem("q8_done"))
        qT_done, qT_copied, f_done, y8_done, out_done = (sem("qT_done"), sem("qT_copied"), sem("f_done"),
                                                         sem("y8_done"), sem("out_done"))

        def chunk(t, i, k):
            return t[:, bass.ds(i * D + k * P, P)]

        def block_of(t, i):
            return t[:, bass.ds(i * D, D)]

        def w_block(t, e, k):
            return t[:, bass.ds(e * (K * D) + k * D, D)]

        block = stack.enter_context(nc.Block())

        @block.sync
        def _(sp):
            sp.dma_start(ids_s[:, :], ids).then_inc(ids_loaded, 16)
            for e in range(E):
                sp.dma_start(w32[:, e * K * D:(e + 1) * K * D].rearrange("p (k f) -> p k f", k=K),
                             ctx_t[e].rearrange("(k p) f -> p k f", p=P)).then_inc(w_loaded[e], 16)
            sp.dma_start(wf[:, :].rearrange("p (k f) -> p k f", k=K),
                         wf_t.rearrange("(k p) f -> p k f", p=P)).then_inc(wf_loaded, 16)

        @block.gpsimd
        def _(pool):
            pool.memset(reach[:, 0, :], 1.0).then_inc(pool_fill, 1)
            pool.memset(reach[:, E, :], 0.0).then_inc(pool_fill, 1)
            pool.memset(scan_one[:, :], 1.0).then_inc(pool_fill, 1)
            pool.memset(row_cum[:, 0:1], 0.0).then_inc(pool_fill, 1)
            pool.memset(ident[:, :], 0.0).then_inc(pool_fill, 1)
            pool.memset(below[:, :], 1.0).then_inc(pool_fill, 1)
            pool.memset(above[:, :], 1.0).then_inc(pool_fill, 1)
            pool.memset(ones_h[:, :], 1.0).then_inc(pool_fill, 1)
            pool.wait_ge(pool_fill, 8)
            pool.affine_select(out=below[:, :], in_=below[:, :], compare_op=ALU.is_gt, fill=0.0, base=0,
                               pattern=[[1, P]], channel_multiplier=-1).then_inc(pool_const, 1)
            pool.affine_select(out=above[:, :], in_=above[:, :], compare_op=ALU.is_gt, fill=0.0, base=0,
                               pattern=[[-1, P]], channel_multiplier=1).then_inc(pool_const, 1)
            pool.iota(iota_q[:, :], [[1, P]], base=0, channel_multiplier=0,
                      allow_small_or_imprecise_dtypes=True).then_inc(pool_const, 1)
            pool.iota(token_no[:, :], [[1, C]], base=0, channel_multiplier=C,
                      allow_small_or_imprecise_dtypes=True).then_inc(pool_const, 1)
            pool.iota(iota_tile[:, :, :], [[0, C], [1, TILES]], base=0, channel_multiplier=0,
                      allow_small_or_imprecise_dtypes=True).then_inc(pool_const, 1)
            pool.iota(iota_job[:, :], [[1, JOBS]], base=0, channel_multiplier=0,
                      allow_small_or_imprecise_dtypes=True).then_inc(pool_const, 1)
            pool.iota(iota_slot[:, :], [[P, JOBS]], base=0, channel_multiplier=1,
                      allow_small_or_imprecise_dtypes=True).then_inc(pool_const, 1)
            pool.affine_select(out=ident[:, :], in_=ident[:, :], compare_op=ALU.not_equal, fill=1.0, base=0,
                               pattern=[[-1, P]], channel_multiplier=1).then_inc(pool_const, 1)
            pool.memset(minus_half[:, :], -0.5).then_inc(pool_const, 1)
            pool.memset(ones_r[:, :], 1.0).then_inc(pool_const, 1)
            pool.wait_ge(pool_const, 10)
            pool.tensor_copy(ident_bf[:, :], ident[:, :]).then_inc(pool_const, 1)

            def gather(i):
                pool.indirect_dma_start(block_of(x1, i), None, x,
                                        bass.IndirectOffsetOnAxis(ap=token_of[:, i:i + 1], axis=0),
                                        bounds_check=T - 1).then_inc(x_gathered[i], 16)

            def rstd_first(i):
                pool.wait_ge(var1_done, i + 1)
                if not isinstance(i, int) or i > 0:
                    pool.wait_ge(h_done, i)
                pool.tensor_tensor(rstd1[:, :], var1[:, :], minus_half[:, :], ALU.pow)\
                    .then_inc(rstd1_done, 1)

            def rstd_second(i):
                pool.wait_ge(var2_done, i + 1)
                if not isinstance(i, int) or i > 0:
                    pool.wait_ge(h2_done, i)
                pool.tensor_tensor(rstd2[:, :], var2[:, :], minus_half[:, :], ALU.pow)\
                    .then_inc(rstd2_done, 1)

            def store_tile(i):
                pool.wait_ge(out_done, i + 1)
                pool.indirect_dma_start(out, bass.IndirectOffsetOnAxis(ap=token_of[:, i:i + 1], axis=0),
                                        block_of(x1, i), None, bounds_check=T - 1).then_inc(stored, 16)

            pool.wait_ge(tokens_ready, 1)
            after_gather = {3: 0, 5: 1, 9: 2, 13: 3}
            for i in range(TILES):
                gather(i)
                if i in after_gather:
                    rstd_first(after_gather[i])
            rstd_first(4)
            pool.wait_ge(wfm_done, 1)
            for k in range(K):
                cols = slice(k * D, (k + 1) * D)
                pool.tensor_tensor(wf_v[:, cols], wf_v[:, cols], wf_m[:, cols], ALU.add).then_inc(wft_done, 1)
                pool.wait_ge(wft_done, k + 1)
                pool.tensor_tensor(wf_q[:, cols], wf_v[:, cols], wf_m[:, cols], ALU.subtract).then_inc(wfq_done, 1)
                if k % 2 == 1:
                    rstd_first(5 + k // 2)
            with pool.Fori(E + 3, TILES) as i:
                rstd_first(i)
                rstd_second(i - E - 3)
            for i in range(TILES - E - 3, TILES):
                rstd_second(i)
            for i in range(TILES):
                pool.wait_ge(vt_done, i + 1)
                if i >= 2:
                    pool.wait_ge(qT_done, i - 1)
                pool.tensor_tensor(q8[:, i % 2, :], vt[:, i % 2, :], vm[:, i % 2, :], ALU.subtract)\
                    .then_inc(q8_done, 1)
                if i >= 3:
                    store_tile(i - 3)
            for i in range(TILES - 3, TILES):
                store_tile(i)
            pool.wait_ge(stored, 16 * TILES)

        @block.tensor
        def _(pe):
            pe.wait_ge(pool_const, 2)
            pe.wait_ge(route, 4)
            pe.matmul(base_ps, above[:, :], row_cum[:, 0:E], start=True, stop=False)
            pe.matmul(base_ps, below[:, :], row_cum[:, 1:E + 1], start=False, stop=True).then_inc(sums_done, 1)
            pe.matmul(start_ps, ones_h[:, :], row_cum[:, :], start=True, stop=True).then_inc(sums_done, 1)
            for c in range(C):
                if c % 4 == 0:
                    pe.wait_ge(onehot_done, c + 4)
                mm = pe.matmul(sort_ps, onehot[:, c, :], pick[:, c, :], start=(c == 0), stop=(c == C - 1))
            mm.then_inc(sort_done, 1)
            pe.wait_ge(pool_const, 10)
            pe.wait_ge(wm_step, E + 2)
            pe.transpose(hT_ps[0:2, 0:P], wmax[:, :], ident[:, :]).then_inc(wmax_T, 1)
            pe.wait_ge(wm_step, E + 4)
            pe.matmul(hT_ps[:, P:P + 2], ones_r[:, :], wmax_d[:, :], start=True, stop=True).then_inc(wmax_B, 1)

            def transpose_h(i):
                pe.wait_ge(h_done, i + 1)
                if isinstance(i, int) and i == 0:
                    pe.wait_ge(wm_step, E + 5)
                for k in range(K):
                    mm = pe.transpose(hT_ps[:, k * P:(k + 1) * P], h[:, k * P:(k + 1) * P], ident[:, :])
                mm.then_inc(hT_done, 1)

            def product(ps, lhs_hi, lhs_lo, expert):
                for k in range(K):
                    pe.matmul(ps, lhs_hi(k), w_block(w_hi, expert, k), start=(k == 0), stop=False)
                    pe.matmul(ps, lhs_hi(k), w_block(w_lo, expert, k), start=False, stop=False)
                for k in range(K):
                    mm = pe.matmul(ps, lhs_lo(k), w_block(w_hi, expert, k), start=False, stop=(k == K - 1))
                return mm

            def up(j, tile, expert):
                if not isinstance(j, int) or j < TILES:
                    pe.wait_ge(hT_hi_done, j + 1)
                    pe.wait_ge(hT_lo_done, j + 1)
                if isinstance(j, int) and j < E:
                    pe.wait_ge(w_hi_done, j + 1)
                    pe.wait_ge(w_lo_done, j + 1)
                product(a_ps[:, :], lambda k: chunk(hT_hi, tile, k), lambda k: chunk(hT_lo, tile, k), expert)\
                    .then_inc(a_done, 1)

            def down(j, expert):
                pe.wait_ge(zT_hi_done, j + 1)
                pe.wait_ge(zT_lo_done, j + 1)
                if not isinstance(j, int) or j > 0:
                    pe.wait_ge(x1_done, j)
                product(y_ps[:, :], lambda k: zT_hi[:, k * P:(k + 1) * P], lambda k: zT_lo[:, k * P:(k + 1) * P],
                        expert).then_inc(y_done, 1)

            def transpose_z(j):
                pe.wait_ge(z_done, j + 1)
                for k in range(K):
                    mm = pe.transpose(zT_ps[:, k * P:(k + 1) * P], z[:, k * P:(k + 1) * P], ident[:, :])
                mm.then_inc(zT_done, 1)

            def expert_of(j):
                return pe.value_load(job_expert_i[0:1, bass.ds(j, 1)], min_val=0, max_val=E - 1)

            def tile_of(j):
                return pe.value_load(job_tile_i[0:1, bass.ds(j, 1)], min_val=0, max_val=TILES - 1)

            def job(j):
                tile, expert = tile_of(j), expert_of(j)
                up(j, tile, expert)
                if not isinstance(j, int) or j + 1 < TILES:
                    transpose_h(j + 1)
                if not isinstance(j, int) or j > 0:
                    down(j - 1, expert_of(j - 1))
                transpose_z(j)

            transpose_h(0)
            pe.wait_ge(jobs_ready, 2)
            for j in range(E):
                job(j)
            with pe.Fori(E, TILES - 1) as j:
                job(j)
            for j in range(TILES - 1, JOBS):
                job(j)
            down(JOBS - 1, expert_of(JOBS - 1))

            pe.wait_ge(xm_step, 1)
            pe.transpose(r_ps[0:1, 0:P], xmax[:, :], ident[:, :]).then_inc(xmax_T, 1)
            pe.wait_ge(xm_step, 2)
            pe.matmul(r_ps[:, P:P + 1], ones_r[0:1, :], xmax_g[:, :], start=True, stop=True).then_inc(xmax_B, 1)

            def transpose_q(i):
                pe.wait_ge(q8_done, i + 1)
                if i >= 2:
                    pe.wait_ge(qT_copied, i - 1)
                for k in range(K):
                    mm = pe.transpose(qT_ps[i % 2][:, k * P:(k + 1) * P], q8[:, i % 2, k * P:(k + 1) * P],
                                      ident_bf[:, :])
                mm.then_inc(qT_done, 1)

            pe.wait_ge(pool_const, 11)
            pe.wait_ge(wfq_done, K)
            transpose_q(0)
            for i in range(TILES):
                if i + 1 < TILES:
                    transpose_q(i + 1)
                pe.wait_ge(qT_copied, i + 1)
                if i >= 2:
                    pe.wait_ge(y8_done, i - 1)
                else:
                    pe.wait_ge(x1_done, JOBS)
                for k in range(K):
                    mm = pe.matmul(f_ps[i % 2][:, :], qT[:, i % 2, k * P:(k + 1) * P], wf_q[:, k * D:(k + 1) * D],
                                   start=(k == 0), stop=(k == K - 1))
                mm.then_inc(f_done, 1)

        @block.scalar
        def _(act):
            act.dma_start(g_s[:, 0:1], g_x.partition_broadcast(P)).then_inc(g_loaded, 16)
            act.dma_start(g_s[:, 1:2], g_f.partition_broadcast(P)).then_inc(g_loaded, 16)
            act.wait_ge(g_loaded, 32)
            act.activation(tg[:, :], g_s[:, :], ACT.Tanh).then_inc(tanh_done, 1)

            def hT_high(i):
                act.wait_ge(hT_done, i + 1)
                act.activation(block_of(hT_hi, i), hT_ps[:, :], ACT.Copy).then_inc(hT_hi_done, 1)

            def w_high(e):
                cols = slice(e * K * D, (e + 1) * K * D)
                act.activation(w_hi[:, cols], w32[:, cols], ACT.Copy, scale=s_w[:, :].bitcast(F32))\
                    .then_inc(w_hi_done, 1)

            def silu(j):
                act.wait_ge(a_done, j + 1)
                if not isinstance(j, int) or j > 0:
                    act.wait_ge(z_done, j)
                act.activation(sg[:, :], a_ps[:, :], ACT.Silu, scale=inv_a[:, :].bitcast(F32)).then_inc(silu_done, 1)

            def zT_high(j):
                act.wait_ge(zT_done, j + 1)
                if not isinstance(j, int) or j > 0:
                    act.wait_ge(y_done, j)
                act.activation(zT_hi[:, :], zT_ps[:, :], ACT.Copy).then_inc(zT_hi_done, 1)

            def job(j):
                silu(j)
                if not isinstance(j, int) or j + 1 < TILES:
                    hT_high(j + 1)
                zT_high(j)

            act.wait_ge(w_scales, 4)
            w_high(0)
            hT_high(0)
            w_high(1)
            for j in range(E):
                job(j)
                if j + 2 < E:
                    w_high(j + 2)
                if j == 1:
                    act.wait_ge(wm_step, E + 6)
                    act.activation(wf_v[:, :], wf[:, :], ACT.Copy, scale=wf_inv[:, :]).then_inc(wfv_done, 1)
            with act.Fori(E, TILES - 1) as j:
                job(j)
            for j in range(TILES - 1, JOBS):
                job(j)

            def scaled(i):
                if i >= 2:
                    act.wait_ge(vt_done, i - 1)
                act.activation(v[:, i % 2, :], block_of(h2, i), ACT.Copy, scale=x_inv[:, :]).then_inc(v_done, 1)

            def copy_qT(i):
                act.wait_ge(qT_done, i + 1)
                if i >= 2:
                    act.wait_ge(f_done, i - 1)
                act.activation(qT[:, i % 2, :], qT_ps[i % 2][:, 0:D], ACT.Copy).then_inc(qT_copied, 1)

            def to_bf16(i):
                act.wait_ge(f_done, i + 1)
                if i >= 2:
                    act.wait_ge(out_done, i - 1)
                act.activation(y8[:, i % 2, :], f_ps[i % 2][:, :], ACT.Copy, scale=out_scale[:, :])\
                    .then_inc(y8_done, 1)

            act.wait_ge(xm_step, 4)
            scaled(0)
            scaled(1)
            for i in range(TILES):
                copy_qT(i)
                if i + 2 < TILES:
                    scaled(i + 2)
                to_bf16(i)

        @block.vector
        def _(dve):
            step = [0]

            def routed(ins):
                step[0] += 1
                ins.then_inc(route, 1)
                dve.wait_ge(route, step[0])

            dve.wait_ge(ids_loaded, 16)
            dve.wait_ge(pool_fill, 4)
            for e in range(1, E):
                ins = dve.tensor_scalar(reach[:, e, :], ids_s[:, :], float(e * PER), None, ALU.is_ge)
            routed(ins)
            routed(dve.tensor_tensor(member[:, :, :], reach[:, 0:E, :], reach[:, 1:E + 1, :], ALU.subtract))
            routed(dve.tensor_tensor_scan(count[:, :], scan_one[:, :], member[:, :, :].rearrange("p e c -> p (e c)"),
                                          0.0, ALU.mult, ALU.add))
            routed(dve.tensor_copy(row_cum[:, 1:E + 1], count[:, C - 1:E * C:C]))
            dve.wait_ge(sums_done, 1)
            routed(dve.tensor_tensor(place[:, :, :], count[:, :].rearrange("p (e c) -> p e c", e=E),
                                     base_ps.unsqueeze(2).to_broadcast([P, E, C]), ALU.add))
            routed(dve.tensor_tensor(place[:, :, :], place[:, :, :], member[:, :, :], ALU.mult))
            routed(dve.tensor_reduce(slot_f[:, :], place[:, :, :].rearrange("p e c -> p c e"), AX.X, ALU.add))
            routed(dve.tensor_scalar(slot_i[:, :], slot_f[:, :], -1.0, None, ALU.add))
            dve.tensor_scalar(q_i[:, :], slot_i[:, :], P - 1, None, ALU.bitwise_and)
            routed(dve.tensor_scalar(tile_i[:, :], slot_i[:, :], P.bit_length() - 1, None, ALU.logical_shift_right))
            dve.tensor_copy(q_f[:, :], q_i[:, :])
            routed(dve.tensor_copy(tile_f[:, :], tile_i[:, :]))
            dve.wait_ge(pool_const, 5)
            routed(dve.tensor_tensor(hit[:, :, :], iota_tile[:, :, :],
                                     tile_f[:, :].unsqueeze(2).to_broadcast([P, C, TILES]), ALU.is_equal))
            dve.tensor_tensor(pick[:, :, :], hit[:, :, :], token_no[:, :].unsqueeze(2).to_broadcast([P, C, TILES]),
                              ALU.mult)
            for c in range(C):
                dve.tensor_scalar(onehot[:, c, :], iota_q[:, :], q_f[:, c:c + 1], None, ALU.is_equal)\
                    .then_inc(onehot_done, 1)
            dve.wait_ge(sort_done, 1)
            dve.tensor_copy(token_of[:, :], sort_ps).then_inc(tokens_ready, 1)

            dve.wait_ge(sums_done, 2)
            dve.tensor_copy(start[:, :], start_ps[:, 0:E])
            routed(dve.tensor_copy(start_i[:, :], start_ps[:, 0:E]))
            routed(dve.tensor_scalar(start_i[:, :], start_i[:, :], P.bit_length() - 1, None, ALU.logical_shift_right))
            for e in range(1, E):
                ins = dve.tensor_scalar(bound[:, e:e + 1], start_i[:, e:e + 1], float(TILES - 1), float(e),
                                        ALU.min, ALU.add)
            routed(ins)
            dve.wait_ge(pool_const, 7)
            routed(dve.tensor_scalar(job_e[:, :], iota_job[:, :], bound[:, 1:2], None, ALU.is_ge))
            for e in range(2, E):
                routed(dve.scalar_tensor_tensor(out=job_e[:, :], in0=iota_job[:, :], scalar=bound[:, e:e + 1],
                                                in1=job_e[:, :], op0=ALU.is_ge, op1=ALU.add))
            dve.tensor_copy(job_expert_i[:, :], job_e[0:1, :]).then_inc(jobs_ready, 1)
            dve.tensor_tensor(job_tile_i[:, :], iota_job[0:1, :], job_e[0:1, :], ALU.subtract).then_inc(jobs_ready, 1)
            routed(dve.scalar_tensor_tensor(out=job_slot[:, :], in0=job_e[:, :], scalar=-float(P),
                                            in1=iota_slot[:, :], op0=ALU.mult, op1=ALU.add))
            routed(dve.tensor_scalar(slot_e[:, :], job_slot[:, :], start[:, 1:2], None, ALU.is_ge))
            for e in range(2, E):
                routed(dve.scalar_tensor_tensor(out=slot_e[:, :], in0=job_slot[:, :], scalar=start[:, e:e + 1],
                                                in1=slot_e[:, :], op0=ALU.is_ge, op1=ALU.add))
            routed(dve.tensor_tensor(mask[:, :], slot_e[:, :], job_e[:, :], ALU.is_equal))

            wstep = [0]

            def measured(ins):
                wstep[0] += 1
                ins.then_inc(wm_step, 1)

            for e in range(E):
                dve.wait_ge(w_loaded[e], 16)
                measured(dve.tensor_reduce(wmax_e[:, e:e + 1], w32[:, e * K * D:(e + 1) * K * D], AX.X, ALU.max,
                                           apply_absolute_value=True))
            dve.wait_ge(wf_loaded, 16)
            measured(dve.tensor_reduce(wmax[:, 1:2], wf[:, :], AX.X, ALU.max, apply_absolute_value=True))
            dve.wait_ge(wm_step, E)
            measured(dve.tensor_reduce(wmax[:, 0:1], wmax_e[:, :], AX.X, ALU.max))
            dve.wait_ge(wmax_T, 1)
            measured(dve.tensor_reduce(wmax_g[:, :], hT_ps[0:2, 0:P], AX.X, ALU.max))
            dve.wait_ge(wm_step, wstep[0])
            measured(dve.tensor_scalar(wmax_d[:, :], ident[0:2, 0:2], wmax_g[:, 0:1], None, ALU.mult))
            dve.wait_ge(wmax_B, 1)
            measured(dve.tensor_copy(wmax_b[:, :], hT_ps[:, P:P + 2]))
            dve.wait_ge(wm_step, wstep[0])
            dve.tensor_scalar(wf_scale[:, :], wmax_b[:, 1:2], 1.0 / E4M3_MAX, 1e-12, ALU.mult, ALU.max)\
                .then_inc(w_scales, 1)
            routed(dve.tensor_scalar(wexp[:, :], wmax_b[:, 0:1].bitcast(I32), EXP_MASK, None, ALU.bitwise_and))
            routed(dve.tensor_scalar(wexp[:, :], wexp[:, :], float((BIAS - W_EXP) * ONE), float((BIAS + W_EXP) * ONE),
                                     ALU.max, ALU.min))
            dve.tensor_scalar(s_w[:, :], wexp[:, :], -1.0, float((2 * BIAS + 13) * ONE), ALU.mult, ALU.add)\
                .then_inc(w_scales, 1)
            dve.tensor_scalar(inv_a[:, :], wexp[:, :], float(-(13 + H_SHIFT) * ONE), None, ALU.add)\
                .then_inc(w_scales, 1)
            dve.tensor_scalar(z_mul[:, :], wexp[:, :], -1.0, float((2 * BIAS - 18 - H_SHIFT) * ONE), ALU.mult,
                              ALU.add).then_inc(w_scales, 1)
            dve.wait_ge(w_scales, 4)
            routed(dve.tensor_scalar(inv_y[:, :], wexp[:, :], 3.0, float((-2 * BIAS - 8) * ONE), ALU.mult, ALU.add))
            dve.wait_ge(tanh_done, 1)
            routed(dve.tensor_tensor(y_mul[:, :], inv_y[:, :].bitcast(F32), tg[:, 0:1], ALU.mult))
            routed(dve.tensor_scalar(job_mul[:, :], mask[:, :], y_mul[:, 0:1], None, ALU.mult))
            measured(dve.reciprocal(wf_inv[:, :], wf_scale[:, :]))

            def w_low(e):
                cols = slice(e * K * D, (e + 1) * K * D)
                dve.wait_ge(w_hi_done, e + 1)
                dve.scalar_tensor_tensor(out=w_lo[:, cols], in0=w32[:, cols], scalar=s_w[:, :].bitcast(F32),
                                         in1=w_hi[:, cols], op0=ALU.mult, op1=ALU.subtract).then_inc(w_lo_done, 1)

            def stats_first(i):
                if isinstance(i, int):
                    dve.wait_ge(x_gathered[i], 16)
                dve.bn_stats(bn1[:, :], block_of(x1, i)).then_inc(bn1_done, 1)

            def var_first(i):
                dve.bn_aggr(mv1[:, :], bn1[:, :]).then_inc(mv1_done, 1)
                dve.wait_ge(mv1_done, i + 1)
                dve.tensor_scalar(var1[:, :], mv1[:, 1:2], EPS, 0.25 ** H_SHIFT, ALU.add, ALU.mult)\
                    .then_inc(var1_done, 1)

            def norm_first(i):
                dve.wait_ge(rstd1_done, i + 1)
                dve.tensor_scalar(h[:, :], block_of(x1, i), mv1[:, 0:1], rstd1[:, :],
                                  ALU.subtract, ALU.mult).then_inc(h_done, 1)

            def hT_low(i):
                dve.wait_ge(hT_hi_done, i + 1)
                dve.tensor_tensor(block_of(hT_lo, i), hT_ps[:, :], block_of(hT_hi, i), ALU.subtract)\
                    .then_inc(hT_lo_done, 1)

            def z_of(j):
                dve.wait_ge(silu_done, j + 1)
                if not isinstance(j, int) or j > 0:
                    dve.wait_ge(zT_done, j)
                dve.scalar_tensor_tensor(out=z[:, :], in0=a_ps[:, :], scalar=z_mul[:, :].bitcast(F32), in1=sg[:, :],
                                         op0=ALU.mult, op1=ALU.mult).then_inc(z_done, 1)

            def zT_low(j):
                dve.wait_ge(zT_hi_done, j + 1)
                dve.tensor_tensor(zT_lo[:, :], zT_ps[:, :], zT_hi[:, :], ALU.subtract).then_inc(zT_lo_done, 1)

            def add_y(j):
                tile = dve.value_load(job_tile_i[0:1, bass.ds(j, 1)], min_val=0, max_val=TILES - 1)
                dve.wait_ge(y_done, j + 1)
                if not isinstance(j, int) or j > 0:
                    dve.wait_ge(x1_done, j)
                dve.scalar_tensor_tensor(out=block_of(x1, tile), in0=y_ps[:, :], scalar=job_mul[:, bass.ds(j, 1)],
                                         in1=block_of(x1, tile), op0=ALU.mult, op1=ALU.add).then_inc(x1_done, 1)

            def stats_second(i):
                dve.wait_ge(x1_done, i + E)
                dve.bn_stats(bn2[:, :], block_of(x1, i)).then_inc(bn2_done, 1)

            def var_second(i):
                dve.bn_aggr(mv2[:, :], bn2[:, :]).then_inc(mv2_done, 1)
                dve.wait_ge(mv2_done, i + 1)
                dve.tensor_scalar(var2[:, :], mv2[:, 1:2], EPS, None, ALU.add).then_inc(var2_done, 1)

            def norm_second(i):
                dve.wait_ge(rstd2_done, i + 1)
                dve.tensor_scalar(block_of(h2, i), block_of(x1, i), mv2[:, 0:1], rstd2[:, :],
                                  ALU.subtract, ALU.mult).then_inc(h2_done, 1)

            def max_second(i):
                dve.wait_ge(h2_done, i + 1)
                dve.tensor_reduce(rmax[:, bass.ds(i, 1)], block_of(h2, i), AX.X, ALU.max, apply_absolute_value=True)\
                    .then_inc(rmax_done, 1)

            def job(j):
                fixed = isinstance(j, int)
                if not fixed or j < JOBS:
                    z_of(j)
                if not fixed or j + 1 < TILES:
                    hT_low(j + 1)
                if not fixed or j + 2 < TILES:
                    norm_first(j + 2)
                if not fixed or j + 3 < TILES:
                    stats_first(j + 3)
                    dve.wait_ge(bn1_done, j + 4)
                    dve.wait_ge(h_done, j + 3)
                if not fixed or j < JOBS:
                    zT_low(j)
                if not fixed or j + 3 < TILES:
                    var_first(j + 3)
                if not fixed or 1 <= j <= JOBS:
                    add_y(j - 1)
                if not fixed or E <= j < TILES + E:
                    stats_second(j - E)
                    dve.wait_ge(bn2_done, j - E + 1)
                if not fixed or j > E:
                    norm_second(j - E - 1)
                if not fixed or j > E:
                    max_second(j - E - 1)
                if not fixed or E <= j < TILES + E:
                    var_second(j - E)

            stats_first(0)
            dve.wait_ge(bn1_done, 1)
            var_first(0)
            w_low(0)
            norm_first(0)
            stats_first(1)
            dve.wait_ge(bn1_done, 2)
            var_first(1)
            hT_low(0)
            norm_first(1)
            w_low(1)
            stats_first(2)
            dve.wait_ge(bn1_done, 3)
            var_first(2)
            for j in range(E + 1):
                job(j)
                if j + 2 < E:
                    w_low(j + 2)
                if j == 2:
                    dve.wait_ge(wfv_done, 1)
                    dve.tensor_scalar(wf_e[:, :].bitcast(I16), wf_v[:, :].bitcast(I16)[:, 1::2], EXP_MASK >> 16, None,
                                      ALU.bitwise_and).then_inc(wfe_done, 1)
                    dve.wait_ge(wfe_done, 1)
                    dve.tensor_scalar(wf_m[:, :], wf_e[:, :], 2.0 ** -6, 1.5 * 2.0 ** 20, ALU.max, ALU.mult)\
                        .then_inc(wfm_done, 1)
            for i in range(E + 4, TILES):
                dve.wait_ge(x_gathered[i], 16)
            with dve.Fori(E + 1, TILES - 3) as j:
                job(j)
            for j in range(TILES - 3, TILES + E + 1):
                job(j)

            dve.wait_ge(rmax_done, TILES)
            dve.tensor_reduce(xmax[:, :], rmax[:, :], AX.X, ALU.max).then_inc(xm_step, 1)
            dve.wait_ge(xmax_T, 1)
            dve.tensor_reduce(xmax_g[:, :], r_ps[0:1, 0:P], AX.X, ALU.max).then_inc(xm_step, 1)
            dve.wait_ge(xmax_B, 1)
            routed(dve.tensor_scalar(x_scale[:, :], r_ps[:, P:P + 1], 1.0 / E4M3_MAX, 1e-12, ALU.mult, ALU.max))
            dve.reciprocal(x_inv[:, :], x_scale[:, :]).then_inc(xm_step, 1)
            dve.tensor_tensor(out_scale[:, :], x_scale[:, :], wf_scale[:, :], ALU.mult).then_inc(xm_step, 1)

            def round_first(i):
                b = i % 2
                dve.wait_ge(v_done, i + 1)
                dve.tensor_scalar(ve[:, b, :].bitcast(I16), v[:, b, :].bitcast(I16)[:, 1::2], EXP_MASK >> 16, None,
                                  ALU.bitwise_and).then_inc(ve_done, 1)
                dve.wait_ge(ve_done, i + 1)
                if i >= 2:
                    dve.wait_ge(q8_done, i - 1)
                dve.tensor_scalar(vm[:, b, :], ve[:, b, :], 2.0 ** -6, 1.5 * 2.0 ** 20, ALU.max, ALU.mult)\
                    .then_inc(vm_done, 1)
                dve.wait_ge(vm_done, i + 1)
                dve.tensor_tensor(vt[:, b, :], v[:, b, :], vm[:, b, :], ALU.add).then_inc(vt_done, 1)

            def finish(i):
                dve.wait_ge(y8_done, i + 1)
                dve.scalar_tensor_tensor(out=block_of(x1, i), in0=y8[:, i % 2, :], scalar=tg[:, 1:2],
                                         in1=block_of(x1, i), op0=ALU.mult, op1=ALU.add).then_inc(out_done, 1)

            for i in range(TILES + 2):
                if i < TILES:
                    round_first(i)
                if i >= 2:
                    finish(i - 2)


def kernel(**inputs):
    import numpy as _np
    import concourse.bacc as _bacc
    from concourse import mybir as _mybir
    from concourse.bass_utils import run_bass_kernel_spmd as _run

    nc = _bacc.Bacc("TRN2", target_bir_lowering=False, num_devices=1)
    a = {k: _np.asarray(v) for k, v in inputs.items()}
    B, S, D = a["x"].shape
    arrays = {
        "in_x": _np.ascontiguousarray(a["x"].reshape(B * S, D)),
        "in_ids": _np.ascontiguousarray(a["itok_BxS_13_99985"].reshape(P, B * S // P)),
        "in_ctx_t": _np.ascontiguousarray(a["ctx_2048"].transpose(0, 2, 1)),
        "in_g_x": _np.ascontiguousarray(a["g_xattn"].reshape(1)),
        "in_g_f": _np.ascontiguousarray(a["g_ffn"].reshape(1)),
        "in_wf_t": _np.ascontiguousarray(a["L0_ffn_weight"].T),
    }
    args = [nc.dram_tensor(n, v.shape, _mybir.dt.from_np(v.dtype), kind="ExternalInput").ap()
            for n, v in arrays.items()]
    args.append(nc.dram_tensor("out_0", (B * S, D), _mybir.dt.float32, kind="ExternalOutput").ap())
    gated_experts_kernel(nc, *args)
    r = _run(nc, [arrays], core_ids=[0])
    return r.results[0]["out_0"].reshape(B, S, D)
```

```python
from contextlib import ExitStack

import concourse.bass as bass
from concourse import mybir

ALU = mybir.AluOpType
ACT = mybir.ActivationFunctionType
AX = mybir.AxisListType
F32 = mybir.dt.float32
F16 = mybir.dt.float16
BF16 = mybir.dt.bfloat16
I32 = mybir.dt.int32
I16 = mybir.dt.int16

P = 128
VOCAB = 25000
EPS = 1e-5
H_SHIFT = 10
EXP_MASK = 0x7F800000
ONE = 1 << 23
BIAS = 127
ROW_MIN, ROW_MAX = 34, 104
NB = 4
E4M3_MAX = 448.0


def gated_experts_kernel(nc, x, ids, ctx_t, g_x, g_f, wf_t, out):
    T, D = x.shape
    E = ctx_t.shape[0]
    K = D // P
    TILES = T // P
    JOBS = TILES + E - 1
    C = ids.shape[1]
    PER = VOCAB // E
    assert ids.shape == (P, C) and P * C == T and D * 4 == 2048

    with ExitStack() as stack:
        def sb(name, shape, dt):
            return stack.enter_context(nc.sbuf_tensor(name, shape, dt))

        def psum(name, shape, dt):
            return stack.enter_context(nc.psum_tensor(name, shape, dt))

        def sem(name):
            return stack.enter_context(nc.semaphore(name))

        ident = sb("ident", [P, P], F32)
        ident_bf = sb("ident_bf", [P, P], BF16)
        below = sb("below", [P, P], F16)
        above = sb("above", [P, P], F16)
        ones_h = sb("ones_h", [P, P], F16)
        ones_bf = sb("ones_bf", [P, P], BF16)
        ones_f = sb("ones_f", [P, P], F32)
        scale_coef = sb("scale_coef", [P, 4], F32)
        scale_off = sb("scale_off", [P, 4], F32)
        iota_q = sb("iota_q", [P, P], F16)
        iota_tile = sb("iota_tile", [P, C, TILES], F32)
        token_no = sb("token_no", [P, C], F32)
        iota_job = sb("iota_job", [P, JOBS], F32)
        iota_slot = sb("iota_slot", [P, JOBS], F32)
        minus_half = sb("minus_half", [P, 1], F32)
        ids_s = sb("ids_s", [P, C], I32)
        reach = sb("reach", [P, E + 1, C], F32)
        member = sb("member", [P, E, C], F32)
        scan_one = sb("scan_one", [P, E * C], F32)
        count = sb("count", [P, E * C], F32)
        row_cum = sb("row_cum", [P, E + 1], F16)
        place = sb("place", [P, E, C], F32)
        slot_f = sb("slot_f", [P, C], F32)
        slot_i = sb("slot_i", [P, C], I32)
        q_i = sb("q_i", [P, C], I32)
        q_h = sb("q_h", [P, C], F16)
        tile_i = sb("tile_i", [P, C], I32)
        tile_f = sb("tile_f", [P, C], F32)
        hit = sb("hit", [P, C, TILES], F32)
        pick = sb("pick", [P, C, TILES], F16)
        onehot = sb("onehot", [P, C, P], F16)
        token_of = sb("token_of", [P, TILES], I32)
        start = sb("start", [P, E], F32)
        start_i = sb("start_i", [P, E], I32)
        bound = sb("bound", [P, E], F32)
        job_e = sb("job_e", [P, JOBS], F32)
        job_slot = sb("job_slot", [P, JOBS], F32)
        slot_e = sb("slot_e", [P, JOBS], F32)
        mask = sb("mask", [P, JOBS], F32)
        job_expert_i = sb("job_expert_i", [1, JOBS], I32)
        job_tile_i = sb("job_tile_i", [1, JOBS], I32)
        g_s = sb("g_s", [P, 2], F32)
        tg = sb("tg", [P, 2], F32)
        row_sq = sb("row_sq", [P, E], F32)
        half_i = sb("half_i", [P, E], I32)
        half_f = sb("half_f", [P, E], F32)
        w_bits = sb("w_bits", [P, E, 4], I32)
        job_is = sb("job_is", [P, E, JOBS], F32)
        table_loaded = sb("table_loaded", [P, 1], F32)
        job_of = sb("job_of", [P, E, JOBS], F32)
        job_inv_a = sb("job_inv_a", [P, JOBS], F32)
        job_z_mul = sb("job_z_mul", [P, JOBS], F32)
        job_mul = sb("job_mul", [P, JOBS], F32)
        diag = sb("diag", [P, P], F32)
        wf_max = sb("wf_max", [P, 2], F32)
        wf_scale = sb("wf_scale", [P, 1], F32)
        wf_inv = sb("wf_inv", [P, 1], F32)
        rmax = sb("rmax", [P, TILES], F32)
        xmax = sb("xmax", [P, 2], F32)
        x_scale = sb("x_scale", [P, 1], F32)
        x_inv = sb("x_inv", [P, 1], F32)
        out_scale = sb("out_scale", [P, 1], F32)
        x1 = sb("x1", [P, TILES * D], F32)
        w32 = sb("w32", [P, E * K * D], F32)
        h2 = w32
        w_hi = sb("w_hi", [P, E * K * D], F16)
        w_lo = sb("w_lo", [P, E * K * D], F16)
        hT_hi = sb("hT_hi", [P, TILES * D], F16)
        hT_lo = sb("hT_lo", [P, TILES * D], F16)
        h = sb("h", [P, D], F32)
        sg = sb("sg", [P, D], F32)
        z = sb("z", [P, D], F32)
        zT_hi = sb("zT_hi", [P, D], F16)
        zT_lo = sb("zT_lo", [P, D], F16)
        bn1 = sb("bn1", [P, 6], F32)
        mv1 = sb("mv1", [P, 2], F32)
        var1 = sb("var1", [P, 1], F32)
        rstd1 = sb("rstd1", [P, 1], F32)
        nmr1 = sb("nmr1", [P, 1], F32)
        bn2 = sb("bn2", [P, 6], F32)
        mv2 = sb("mv2", [P, 2], F32)
        var2 = sb("var2", [P, 1], F32)
        rstd2 = sb("rstd2", [P, 1], F32)
        nmr2 = sb("nmr2", [P, 1], F32)
        wf = sb("wf", [P, K * D], BF16)
        wf_v = sb("wf_v", [P, K * D], F32)
        wf_e = sb("wf_e", [P, K * D], BF16)
        wf_m = sb("wf_m", [P, K * D], BF16)
        wf_q = sb("wf_q", [P, K * D], BF16)
        v = sb("v", [P, NB, D], BF16)
        vt = w_hi[:, :].bitcast(F32)[:, 0:NB * D].rearrange("p (b d) -> p b d", b=NB)
        ve = sb("ve", [P, NB, D], BF16)
        vm = sb("vm", [P, NB, D], BF16)
        q8 = sb("q8", [P, NB, D], BF16)
        qT = sb("qT", [P, NB, D], BF16)
        y8 = sb("y8", [P, NB, D], BF16)

        a_ps = psum("a_ps", [P, D], F32)
        y_ps = psum("y_ps", [P, D], F32)
        hT_ps = psum("hT_ps", [P, D], F32)
        zT_ps = psum("zT_ps", [P, D], F32)
        r_ps = psum("r_ps", [P, 512], F32)
        c_ps = psum("c_ps", [P, 512], F32)
        n_ps = psum("n_ps", [P, 512], F32)
        m_ps = psum("m_ps", [P, 512], F32)
        f_ps = [a_ps, y_ps, hT_ps, zT_ps]
        qT_ps = [n_ps[:, :].bitcast(BF16), r_ps[:, :].bitcast(BF16), c_ps[:, :].bitcast(BF16)]
        NQ = len(qT_ps)
        base_ps = r_ps[:, 0:E]
        start_ps = c_ps[:, 64:64 + E + 1]
        sort_ps = c_ps[:, 0:TILES]

        ids_loaded, g_loaded, wf_loaded = sem("ids_loaded"), sem("g_loaded"), sem("wf_loaded")
        w_loaded = [sem(f"w_loaded{e}") for e in range(E)]
        x_gathered = [sem(f"x_gathered{i}") for i in range(TILES)]
        stored = sem("stored")
        pool_const, pool_fill = sem("pool_const"), sem("pool_fill")
        route = sem("route")
        sums_done, sort_done = sem("sums_done"), sem("sort_done")
        onehot_done = sem("onehot_done")
        tokens_ready, jobs_ready = sem("tokens_ready"), sem("jobs_ready")
        tanh_done = sem("tanh_done")
        squares_done, norms_done, norms_read = sem("squares_done"), sem("norms_done"), sem("norms_read")
        w_scales, job_scales = sem("w_scales"), sem("job_scales")
        wfs_done = sem("wfs_done")
        wf_step, wf_max_done, wf_scaled = sem("wf_step"), sem("wf_max_done"), sem("wf_scaled")
        nmr1_done, nmr2_done = sem("nmr1_done"), sem("nmr2_done")
        w_hi_done, w_lo_done = sem("w_hi_done"), sem("w_lo_done")
        bn1_done, mv1_done, var1_done, rstd1_done = sem("bn1_done"), sem("mv1_done"), sem("var1_done"), sem("rstd1_done")
        bn2_done, mv2_done, var2_done, rstd2_done = sem("bn2_done"), sem("mv2_done"), sem("var2_done"), sem("rstd2_done")
        h_done, hT_done = sem("h_done"), sem("hT_done")
        hT_hi_done, hT_lo_done = sem("hT_hi_done"), sem("hT_lo_done")
        a_done, silu_done, z_done, zT_done = sem("a_done"), sem("silu_done"), sem("z_done"), sem("zT_done")
        zT_hi_done, zT_lo_done, y_done, x1_done = sem("zT_hi_done"), sem("zT_lo_done"), sem("y_done"), sem("x1_done")
        h2_done, rmax_done = sem("h2_done"), sem("rmax_done")
        wfv_done, wfe_done, wfm_done, wft_done, wfq_done = (sem("wfv_done"), sem("wfe_done"), sem("wfm_done"),
                                                            sem("wft_done"), sem("wfq_done"))
        xm_step, xmax_done = sem("xm_step"), sem("xmax_done")
        v_done, ve_done, vm_done, vt_done = sem("v_done"), sem("ve_done"), sem("vm_done"), sem("vt_done")
        q8_done = [sem(f"q8_done{i}") for i in range(TILES)]
        qT_done, qT_copied, f_done, y8_done, out_done = (sem("qT_done"), sem("qT_copied"), sem("f_done"),
                                                         sem("y8_done"), sem("out_done"))

        M_OFF = 64 - BIAS
        SCALES = [(-1, BIAS + 15 - M_OFF),
                  (1, BIAS - 15 - H_SHIFT + M_OFF),
                  (-1, BIAS - 15 - H_SHIFT + 5 - M_OFF),
                  (3, BIAS - 15 - 5 + 3 * M_OFF)]
        S_W, INV_A, Z_MUL, INV_Y = range(4)

        def w_scale(e, n):
            return w_bits[:, e, n:n + 1].bitcast(F32)

        def chunk(t, i, k):
            return t[:, bass.ds(i * D + k * P, P)]

        def block_of(t, i):
            return t[:, bass.ds(i * D, D)]

        def w_block(t, e, k):
            return t[:, bass.ds(e * (K * D) + k * D, D)]

        STORE_LAG = 4

        def on_pool(i):
            return i % 4 != 3

        block = stack.enter_context(nc.Block())

        @block.sync
        def _(sp):
            sp.dma_start(ids_s[:, :], ids).then_inc(ids_loaded, 16)
            for e in range(E):
                if e == 2:
                    sp.wait_ge(x_gathered[1], 16)
                sp.dma_start(w32[:, e * K * D:(e + 1) * K * D].rearrange("p (k f) -> p k f", k=K),
                             ctx_t[e].rearrange("(k p) f -> p k f", p=P)).then_inc(w_loaded[e], 16)
            sp.dma_start(wf[:, :].rearrange("p (k f) -> p k f", k=K),
                         wf_t.rearrange("(k p) f -> p k f", p=P)).then_inc(wf_loaded, 16)

        @block.gpsimd
        def _(pool):
            pool.memset(reach[:, 0, :], 1.0).then_inc(pool_fill, 1)
            pool.memset(reach[:, E, :], 0.0).then_inc(pool_fill, 1)
            pool.memset(scan_one[:, :], 1.0).then_inc(pool_fill, 1)
            pool.memset(row_cum[:, 0:1], 0.0).then_inc(pool_fill, 1)
            pool.memset(ident[:, :], 0.0).then_inc(pool_fill, 1)
            pool.memset(below[:, :], 1.0).then_inc(pool_fill, 1)
            pool.memset(above[:, :], 1.0).then_inc(pool_fill, 1)
            pool.memset(ones_h[:, :], 1.0).then_inc(pool_fill, 1)
            pool.wait_ge(pool_fill, 8)
            pool.affine_select(out=below[:, :], in_=below[:, :], compare_op=ALU.is_gt, fill=0.0, base=0,
                               pattern=[[1, P]], channel_multiplier=-1).then_inc(pool_const, 1)
            pool.affine_select(out=above[:, :], in_=above[:, :], compare_op=ALU.is_gt, fill=0.0, base=0,
                               pattern=[[-1, P]], channel_multiplier=1).then_inc(pool_const, 1)
            pool.iota(iota_q[:, :], [[1, P]], base=0, channel_multiplier=0,
                      allow_small_or_imprecise_dtypes=True).then_inc(pool_const, 1)
            pool.iota(token_no[:, :], [[1, C]], base=0, channel_multiplier=C,
                      allow_small_or_imprecise_dtypes=True).then_inc(pool_const, 1)
            pool.iota(iota_tile[:, :, :], [[0, C], [1, TILES]], base=0, channel_multiplier=0,
                      allow_small_or_imprecise_dtypes=True).then_inc(pool_const, 1)
            pool.iota(iota_job[:, :], [[1, JOBS]], base=0, channel_multiplier=0,
                      allow_small_or_imprecise_dtypes=True).then_inc(pool_const, 1)
            pool.iota(iota_slot[:, :], [[P, JOBS]], base=0, channel_multiplier=1,
                      allow_small_or_imprecise_dtypes=True).then_inc(pool_const, 1)
            pool.affine_select(out=ident[:, :], in_=ident[:, :], compare_op=ALU.not_equal, fill=1.0, base=0,
                               pattern=[[-1, P]], channel_multiplier=1).then_inc(pool_const, 1)
            pool.memset(minus_half[:, :], -0.5).then_inc(pool_const, 1)
            pool.memset(ones_bf[:, :], 1.0).then_inc(pool_const, 1)
            for n, (coef, off) in enumerate(SCALES):
                pool.memset(scale_coef[:, n:n + 1], float(coef))
                ins = pool.memset(scale_off[:, n:n + 1], float(off * ONE))
            ins.then_inc(pool_const, 1)
            pool.memset(ones_f[:, :], 1.0).then_inc(pool_const, 1)
            pool.wait_ge(pool_const, 12)
            pool.tensor_copy(ident_bf[:, :], ident[:, :]).then_inc(pool_const, 1)

            def gather(i):
                pool.indirect_dma_start(block_of(x1, i), None, x,
                                        bass.IndirectOffsetOnAxis(ap=token_of[:, i:i + 1], axis=0),
                                        bounds_check=T - 1).then_inc(x_gathered[i], 16)

            def rstd_first(i):
                pool.wait_ge(var1_done, i + 1)
                if not isinstance(i, int) or i > 0:
                    pool.wait_ge(h_done, i)
                    pool.wait_ge(nmr1_done, i)
                pool.tensor_tensor(rstd1[:, :], var1[:, :], minus_half[:, :], ALU.pow)\
                    .then_inc(rstd1_done, 1)

            def rstd_second(i):
                pool.wait_ge(var2_done, i + 1)
                if not isinstance(i, int) or i > 0:
                    pool.wait_ge(h2_done, i)
                    pool.wait_ge(nmr2_done, i)
                pool.tensor_tensor(rstd2[:, :], var2[:, :], minus_half[:, :], ALU.pow)\
                    .then_inc(rstd2_done, 1)

            def store_tile(i):
                pool.wait_ge(out_done, i + 1)
                pool.indirect_dma_start(out, bass.IndirectOffsetOnAxis(ap=token_of[:, i:i + 1], axis=0),
                                        block_of(x1, i), None, bounds_check=T - 1).then_inc(stored, 16)

            def job(j):
                if not isinstance(j, int) or j + 2 < TILES:
                    rstd_first(j + 2)
                if not isinstance(j, int) or j >= E:
                    rstd_second(j - E)

            pool.wait_ge(tokens_ready, 1)
            after_gather = {4: 0, 7: 1, 13: 2}
            for i in range(TILES):
                gather(i)
                if i in after_gather:
                    rstd_first(after_gather[i])
            for j in range(1, E + 1):
                job(j)
            with pool.Fori(E + 1, TILES - 2) as j:
                job(j)
            for j in range(TILES - 2, TILES + E):
                job(j)
                if j == JOBS - 2:
                    pool.wait_ge(wfm_done, 1)
                    for k in range(K // 2):
                        cols = slice(k * D, (k + 1) * D)
                        pool.tensor_tensor(wf_v[:, cols], wf_v[:, cols], wf_m[:, cols], ALU.add).then_inc(wft_done, 1)
                        pool.wait_ge(wft_done, k + 1)
                        pool.tensor_tensor(wf_q[:, cols], wf_v[:, cols], wf_m[:, cols], ALU.subtract)\
                            .then_inc(wfq_done, 1)
            for i in range(TILES):
                if on_pool(i):
                    pool.wait_ge(vt_done, i + 1)
                    if i >= NB:
                        pool.wait_ge(qT_done, i - NB + 1)
                    pool.tensor_tensor(q8[:, i % NB, :], vt[:, i % NB, :], vm[:, i % NB, :], ALU.subtract)\
                        .then_inc(q8_done[i], 1)
                if i >= STORE_LAG:
                    store_tile(i - STORE_LAG)
            for i in range(TILES - STORE_LAG, TILES):
                store_tile(i)
            pool.wait_ge(stored, 16 * TILES)

        @block.tensor
        def _(pe):
            pe.wait_ge(pool_const, 2)
            pe.wait_ge(route, 4)
            pe.matmul(base_ps, above[:, :], row_cum[:, 0:E], start=True, stop=False)
            pe.matmul(base_ps, below[:, :], row_cum[:, 1:E + 1], start=False, stop=True).then_inc(sums_done, 1)
            pe.matmul(start_ps, ones_h[:, :], row_cum[:, :], start=True, stop=True).then_inc(sums_done, 1)
            def row_norms(e, k):
                if k == 0 and e > 0:
                    pe.wait_ge(norms_read, e)
                pe.wait_ge(squares_done, K * e + k + 1)
                mm = pe.matmul(n_ps[:, :], ones_bf[:, :], w_block(w_lo, e, k).bitcast(BF16), start=(k == 0),
                               stop=(k == K - 1))
                if k == K - 1:
                    mm.then_inc(norms_done, 1)

            pe.wait_ge(pool_const, 10)
            for c in range(C):
                if c % 4 == 0:
                    pe.wait_ge(onehot_done, c + 4)
                mm = pe.matmul(sort_ps, onehot[:, c, :], pick[:, c, :], start=(c == 0), stop=(c == C - 1))
                if c == C - 1:
                    mm.then_inc(sort_done, 1)
                if c % 4 == 3:
                    row_norms(0, c // 4)
            def transpose_h(i):
                pe.wait_ge(h_done, i + 1)
                for k in range(K):
                    mm = pe.transpose(hT_ps[:, k * P:(k + 1) * P], h[:, k * P:(k + 1) * P], ident[:, :])
                mm.then_inc(hT_done, 1)

            def product(ps, lhs_hi, lhs_lo, expert, lo_ready, first=None):
                for k in range(K):
                    if first is not None:
                        pe.wait_ge(w_hi_done, K * first + k + 1)
                    pe.matmul(ps, lhs_hi(k), w_block(w_hi, expert, k), start=(k == 0), stop=False)
                if first is not None:
                    lo_ready()
                    for k in range(K):
                        pe.matmul(ps, lhs_lo(k), w_block(w_hi, expert, k), start=False, stop=False)
                for k in range(K):
                    if first is not None:
                        pe.wait_ge(w_lo_done, K * first + k + 1)
                    mm = pe.matmul(ps, lhs_hi(k), w_block(w_lo, expert, k), start=False,
                                   stop=(first is not None and k == K - 1))
                if first is None:
                    lo_ready()
                    for k in range(K):
                        mm = pe.matmul(ps, lhs_lo(k), w_block(w_hi, expert, k), start=False, stop=(k == K - 1))
                return mm

            def up(j, tile, expert):
                loading = not isinstance(j, int) or j < TILES
                if loading:
                    pe.wait_ge(hT_hi_done, j + 1)

                def lo_ready():
                    if loading:
                        pe.wait_ge(hT_lo_done, j + 1)

                product(a_ps[:, :], lambda k: chunk(hT_hi, tile, k), lambda k: chunk(hT_lo, tile, k), expert,
                        lo_ready, j if isinstance(j, int) and j < E else None).then_inc(a_done, 1)

            def down(j, expert):
                pe.wait_ge(zT_hi_done, j + 1)
                if not isinstance(j, int) or j > 0:
                    pe.wait_ge(x1_done, j)
                product(y_ps[:, :], lambda k: zT_hi[:, k * P:(k + 1) * P], lambda k: zT_lo[:, k * P:(k + 1) * P],
                        expert, lambda: pe.wait_ge(zT_lo_done, j + 1)).then_inc(y_done, 1)

            def transpose_z(j):
                pe.wait_ge(z_done, j + 1)
                for k in range(K):
                    mm = pe.transpose(zT_ps[:, k * P:(k + 1) * P], z[:, k * P:(k + 1) * P], ident[:, :])
                mm.then_inc(zT_done, 1)

            def expert_of(j):
                return pe.value_load(job_expert_i[0:1, bass.ds(j, 1)], min_val=0, max_val=E - 1)

            def tile_of(j):
                return pe.value_load(job_tile_i[0:1, bass.ds(j, 1)], min_val=0, max_val=TILES - 1)

            def job(j):
                tile, expert = tile_of(j), expert_of(j)
                up(j, tile, expert)
                if not isinstance(j, int) or j + 1 < TILES:
                    transpose_h(j + 1)
                if isinstance(j, int) and j == 1:
                    for k in range(K):
                        row_norms(2, k)
                if not isinstance(j, int) or j > 0:
                    down(j - 1, expert_of(j - 1))
                transpose_z(j)
                if isinstance(j, int) and j == 1:
                    for k in range(K):
                        row_norms(3, k)

            row_norms(1, 0)
            transpose_h(0)
            for k in range(1, K):
                row_norms(1, k)
            pe.wait_ge(jobs_ready, 2)
            for j in range(E):
                job(j)
            with pe.Fori(E, TILES - 2, 2) as j:
                job(j)
                job(j + 1)
            for j in range(TILES - 2, JOBS):
                job(j)
                if j == TILES - 1:
                    pe.wait_ge(pool_const, 12)
                    pe.wait_ge(wf_step, 2)
                    pe.matmul(m_ps[:, 0:P], ones_f[:, :], diag[:, :], start=True, stop=True).then_inc(wf_max_done, 1)
            down(JOBS - 1, expert_of(JOBS - 1))

            pe.wait_ge(xm_step, 2)
            pe.matmul(m_ps[:, P:2 * P], ones_f[:, :], diag[:, :], start=True, stop=True).then_inc(xmax_done, 1)

            def transpose_q(i):
                pe.wait_ge(q8_done[i], 1)
                if i >= NQ:
                    pe.wait_ge(qT_copied, i - NQ + 1)
                for k in range(K):
                    mm = pe.transpose(qT_ps[i % NQ][:, k * P:(k + 1) * P], q8[:, i % NB, k * P:(k + 1) * P],
                                      ident_bf[:, :])
                mm.then_inc(qT_done, 1)

            pe.wait_ge(pool_const, 13)
            pe.wait_ge(wfq_done, K // 2)
            pe.wait_ge(wfs_done, 2)
            transpose_q(0)
            for i in range(TILES):
                if i + 1 < TILES:
                    transpose_q(i + 1)
                pe.wait_ge(qT_copied, i + 1)
                if i >= NB:
                    pe.wait_ge(y8_done, i - NB + 1)
                for k in range(K):
                    mm = pe.matmul(f_ps[i % NB][:, :], qT[:, i % NB, k * P:(k + 1) * P], wf_q[:, k * D:(k + 1) * D],
                                   start=(k == 0), stop=(k == K - 1))
                mm.then_inc(f_done, 1)

        @block.scalar
        def _(act):
            act.dma_start(g_s[:, 0:1], g_x.partition_broadcast(P)).then_inc(g_loaded, 16)
            act.dma_start(g_s[:, 1:2], g_f.partition_broadcast(P)).then_inc(g_loaded, 16)
            act.wait_ge(pool_fill, 3)
            act.activation(table_loaded[:, :], scan_one[:, 0:1], ACT.Silu)

            def hT_high(i):
                act.wait_ge(hT_done, i + 1)
                act.activation(block_of(hT_hi, i), hT_ps[:, :], ACT.Copy).then_inc(hT_hi_done, 1)

            def squares(e, chunks=range(K)):
                act.wait_ge(w_loaded[e], 16)
                for k in chunks:
                    act.activation(w_block(w_lo, e, k).bitcast(BF16), w_block(w32, e, k), ACT.Square)\
                        .then_inc(squares_done, 1)

            def w_high(e, chunks=range(K)):
                act.wait_ge(w_scales, e + 1)
                for k in chunks:
                    act.activation(w_block(w_hi, e, k), w_block(w32, e, k), ACT.Copy, scale=w_scale(e, S_W))\
                        .then_inc(w_hi_done, 1)

            def norm_first(i):
                act.wait_ge(nmr1_done, i + 1)
                if not isinstance(i, int) or i > 0:
                    act.wait_ge(hT_done, i)
                act.activation(h[:, :], block_of(x1, i), ACT.Identity, bias=nmr1[:, :], scale=rstd1[:, :])\
                    .then_inc(h_done, 1)

            def norm_second(i):
                act.wait_ge(nmr2_done, i + 1)
                act.activation(block_of(h2, i), block_of(x1, i), ACT.Identity, bias=nmr2[:, :], scale=rstd2[:, :])\
                    .then_inc(h2_done, 1)

            def silu(j):
                act.wait_ge(a_done, j + 1)
                if isinstance(j, int) and j < E:
                    act.wait_ge(job_scales, 2 if j == 0 else 3 * (j + 1))
                if not isinstance(j, int) or j > 0:
                    act.wait_ge(z_done, j)
                act.activation(sg[:, :], a_ps[:, :], ACT.Silu, scale=job_inv_a[:, bass.ds(j, 1)]).then_inc(silu_done, 1)

            def zT_high(j):
                act.wait_ge(zT_done, j + 1)
                if not isinstance(j, int) or j > 0:
                    act.wait_ge(y_done, j)
                act.activation(zT_hi[:, :], zT_ps[:, :], ACT.Copy).then_inc(zT_hi_done, 1)

            def job(j):
                fixed = isinstance(j, int)
                if not fixed or j < JOBS:
                    silu(j)
                if not fixed or j + 1 < TILES:
                    hT_high(j + 1)
                if fixed and j == 0:
                    squares(2, range(2))
                if fixed and j == 1:
                    squares(3)
                if fixed and 1 <= j and j + 1 < E:
                    w_high(j + 1, range(2))
                if not fixed or j > E:
                    norm_second(j - E - 1)
                if not fixed or j < JOBS:
                    zT_high(j)
                if fixed and j == 0:
                    squares(2, range(2, K))
                if fixed and 1 <= j and j + 1 < E:
                    w_high(j + 1, range(2, K))
                if not fixed or j + 2 < TILES:
                    norm_first(j + 2)

            squares(0)
            act.wait_ge(g_loaded, 32)
            act.activation(tg[:, :], g_s[:, :], ACT.Tanh).then_inc(tanh_done, 1)
            w_high(0)
            squares(1, range(1))
            norm_first(0)
            squares(1, range(1, K))
            hT_high(0)
            norm_first(1)
            w_high(1)
            for j in range(E + 1):
                job(j)
                if j == E:
                    act.wait_ge(w_lo_done, K * E)
            with act.Fori(E + 1, TILES - 2) as j:
                job(j)
            for j in range(TILES - 2, TILES + E + 1):
                job(j)
                if j == TILES:
                    act.wait_ge(wf_scaled, 1)
                    act.activation(wf_v[:, :], wf[:, :], ACT.Copy, scale=wf_inv[:, :]).then_inc(wfv_done, 1)

            def scaled(i):
                if i >= NB:
                    act.wait_ge(ve_done, i - NB + 1)
                act.activation(v[:, i % NB, :], block_of(h2, i), ACT.Copy, scale=x_inv[:, :]).then_inc(v_done, 1)

            def copy_qT(i):
                act.wait_ge(qT_done, i + 1)
                if i >= NB:
                    act.wait_ge(f_done, i - NB + 1)
                act.activation(qT[:, i % NB, :], qT_ps[i % NQ][:, 0:D], ACT.Copy).then_inc(qT_copied, 1)

            def to_bf16(i):
                act.wait_ge(f_done, i + 1)
                if i >= NB:
                    act.wait_ge(out_done, i - NB + 1)
                act.activation(y8[:, i % NB, :], f_ps[i % NB][:, :], ACT.Copy, scale=out_scale[:, :])\
                    .then_inc(y8_done, 1)

            act.wait_ge(xm_step, 5)
            V_AHEAD, Y_BEHIND = 3, 1
            for i in range(V_AHEAD):
                scaled(i)
            for i in range(TILES + Y_BEHIND):
                if i < TILES:
                    copy_qT(i)
                if i + V_AHEAD < TILES:
                    scaled(i + V_AHEAD)
                if i >= Y_BEHIND:
                    to_bf16(i - Y_BEHIND)

        @block.vector
        def _(dve):
            step = [0]

            def routed(ins):
                step[0] += 1
                ins.then_inc(route, 1)
                dve.wait_ge(route, step[0])

            dve.wait_ge(ids_loaded, 16)
            dve.wait_ge(pool_fill, 4)
            for e in range(1, E):
                ins = dve.tensor_scalar(reach[:, e, :], ids_s[:, :], float(e * PER), None, ALU.is_ge)
            routed(ins)
            routed(dve.tensor_tensor(member[:, :, :], reach[:, 0:E, :], reach[:, 1:E + 1, :], ALU.subtract))
            routed(dve.tensor_tensor_scan(count[:, :], scan_one[:, :], member[:, :, :].rearrange("p e c -> p (e c)"),
                                          0.0, ALU.mult, ALU.add))
            routed(dve.tensor_copy(row_cum[:, 1:E + 1], count[:, C - 1:E * C:C]))
            dve.wait_ge(sums_done, 1)
            routed(dve.tensor_tensor(place[:, :, :], count[:, :].rearrange("p (e c) -> p e c", e=E),
                                     base_ps.unsqueeze(2).to_broadcast([P, E, C]), ALU.add))
            routed(dve.tensor_tensor(place[:, :, :], place[:, :, :], member[:, :, :], ALU.mult))
            routed(dve.tensor_reduce(slot_f[:, :], place[:, :, :].rearrange("p e c -> p c e"), AX.X, ALU.add))
            routed(dve.tensor_scalar(slot_i[:, :], slot_f[:, :], -1.0, None, ALU.add))
            dve.tensor_scalar(q_i[:, :], slot_i[:, :], P - 1, None, ALU.bitwise_and)
            routed(dve.tensor_scalar(tile_i[:, :], slot_i[:, :], P.bit_length() - 1, None, ALU.logical_shift_right))
            dve.tensor_copy(q_h[:, :], q_i[:, :])
            routed(dve.tensor_copy(tile_f[:, :], tile_i[:, :]))
            dve.wait_ge(pool_const, 5)
            routed(dve.tensor_tensor(hit[:, :, :], iota_tile[:, :, :],
                                     tile_f[:, :].unsqueeze(2).to_broadcast([P, C, TILES]), ALU.is_equal))
            dve.tensor_tensor(pick[:, :, :], hit[:, :, :], token_no[:, :].unsqueeze(2).to_broadcast([P, C, TILES]),
                              ALU.mult)
            for c in range(0, C, 4):
                dve.tensor_tensor(onehot[:, c:c + 4, :], iota_q[:, :].unsqueeze(1).to_broadcast([P, 4, P]),
                                  q_h[:, c:c + 4].unsqueeze(2).to_broadcast([P, 4, P]), ALU.is_equal)\
                    .then_inc(onehot_done, 4)
            dve.wait_ge(sort_done, 1)
            dve.tensor_copy(token_of[:, :], sort_ps).then_inc(tokens_ready, 1)

            def w_scaling(e):
                dve.wait_ge(norms_done, e + 1)
                dve.tensor_reduce(row_sq[:, e:e + 1], n_ps[:, :], AX.X, ALU.max).then_inc(norms_read, 1)
                dve.wait_ge(norms_read, e + 1)
                routed(dve.tensor_scalar(half_i[:, e:e + 1], row_sq[:, e:e + 1].bitcast(I32), 1, EXP_MASK,
                                         ALU.logical_shift_right, ALU.bitwise_and))
                routed(dve.tensor_scalar(half_f[:, e:e + 1], half_i[:, e:e + 1], float(ROW_MIN * ONE),
                                         float(ROW_MAX * ONE), ALU.max, ALU.min))
                if e == 0:
                    dve.wait_ge(pool_const, 11)
                dve.scalar_tensor_tensor(out=w_bits[:, e, :], in0=scale_coef[:, :], scalar=half_f[:, e:e + 1],
                                         in1=scale_off[:, :], op0=ALU.mult, op1=ALU.add).then_inc(w_scales, 1)
                dve.wait_ge(w_scales, e + 1)

            dve.wait_ge(sums_done, 2)
            dve.tensor_copy(start[:, :], start_ps[:, 0:E])
            routed(dve.tensor_copy(start_i[:, :], start_ps[:, 0:E]))
            routed(dve.tensor_scalar(start_i[:, :], start_i[:, :], P.bit_length() - 1, None, ALU.logical_shift_right))
            for e in range(1, E):
                ins = dve.tensor_scalar(bound[:, e:e + 1], start_i[:, e:e + 1], float(TILES - 1), float(e),
                                        ALU.min, ALU.add)
            routed(ins)
            dve.wait_ge(pool_const, 7)
            routed(dve.tensor_scalar(job_e[:, :], iota_job[:, :], bound[:, 1:2], None, ALU.is_ge))
            for e in range(2, E):
                routed(dve.scalar_tensor_tensor(out=job_e[:, :], in0=iota_job[:, :], scalar=bound[:, e:e + 1],
                                                in1=job_e[:, :], op0=ALU.is_ge, op1=ALU.add))
            dve.tensor_copy(job_expert_i[:, :], job_e[0:1, :]).then_inc(jobs_ready, 1)
            dve.tensor_tensor(job_tile_i[:, :], iota_job[0:1, :], job_e[0:1, :], ALU.subtract).then_inc(jobs_ready, 1)
            w_scaling(0)
            for e in range(E):
                ins = dve.tensor_scalar(job_is[:, e, :], job_e[:, :], float(e), None, ALU.is_equal)
            routed(ins)
            def job_tables(e, tables=((job_inv_a, job_is, INV_A), (job_z_mul, job_is, Z_MUL),
                                      (job_mul, job_of, INV_Y))):
                if e > 0:
                    dve.wait_ge(job_scales, 3 * e)
                for table, chosen, n in tables:
                    if e == 0:
                        ins = dve.tensor_scalar(table[:, :], chosen[:, 0, :], w_scale(0, n), None, ALU.mult)
                    else:
                        ins = dve.scalar_tensor_tensor(out=table[:, e:], in0=chosen[:, e, e:], scalar=w_scale(e, n),
                                                       in1=table[:, e:], op0=ALU.mult, op1=ALU.add)
                    ins.then_inc(job_scales, 1)

            job_tables(0, ((job_inv_a, job_is, INV_A), (job_z_mul, job_is, Z_MUL)))

            def w_low(e, chunks=range(K)):
                for k in chunks:
                    dve.wait_ge(w_hi_done, K * e + k + 1)
                    dve.scalar_tensor_tensor(out=w_block(w_lo, e, k), in0=w_block(w32, e, k), scalar=w_scale(e, S_W),
                                             in1=w_block(w_hi, e, k), op0=ALU.mult, op1=ALU.subtract)\
                        .then_inc(w_lo_done, 1)

            def stats_first(i):
                if isinstance(i, int):
                    dve.wait_ge(x_gathered[i], 16)
                dve.bn_stats(bn1[:, :], block_of(x1, i)).then_inc(bn1_done, 1)
                dve.wait_ge(bn1_done, i + 1)
                if not isinstance(i, int) or i > 0:
                    dve.wait_ge(nmr1_done, i)

            def var_first(i):
                dve.bn_aggr(mv1[:, :], bn1[:, :]).then_inc(mv1_done, 1)
                dve.wait_ge(mv1_done, i + 1)
                dve.tensor_scalar(var1[:, :], mv1[:, 1:2], EPS, 0.25 ** H_SHIFT, ALU.add, ALU.mult)\
                    .then_inc(var1_done, 1)

            def shift_first(i):
                dve.wait_ge(rstd1_done, i + 1)
                if not isinstance(i, int) or i > 0:
                    dve.wait_ge(h_done, i)
                dve.scalar_tensor_tensor(out=nmr1[:, :], in0=mv1[:, 0:1], scalar=-1.0, in1=rstd1[:, :],
                                         op0=ALU.mult, op1=ALU.mult).then_inc(nmr1_done, 1)

            def hT_low(i):
                dve.wait_ge(hT_hi_done, i + 1)
                dve.tensor_tensor(block_of(hT_lo, i), hT_ps[:, :], block_of(hT_hi, i), ALU.subtract)\
                    .then_inc(hT_lo_done, 1)

            def z_of(j):
                dve.wait_ge(silu_done, j + 1)
                if not isinstance(j, int) or j > 0:
                    dve.wait_ge(zT_done, j)
                dve.scalar_tensor_tensor(out=z[:, :], in0=a_ps[:, :], scalar=job_z_mul[:, bass.ds(j, 1)],
                                         in1=sg[:, :], op0=ALU.mult, op1=ALU.mult).then_inc(z_done, 1)

            def zT_low(j):
                dve.wait_ge(zT_hi_done, j + 1)
                dve.tensor_tensor(zT_lo[:, :], zT_ps[:, :], zT_hi[:, :], ALU.subtract).then_inc(zT_lo_done, 1)

            def add_y(j):
                tile = dve.value_load(job_tile_i[0:1, bass.ds(j, 1)], min_val=0, max_val=TILES - 1)
                dve.wait_ge(y_done, j + 1)
                if not isinstance(j, int) or j > 0:
                    dve.wait_ge(x1_done, j)
                dve.scalar_tensor_tensor(out=block_of(x1, tile), in0=y_ps[:, :], scalar=job_mul[:, bass.ds(j, 1)],
                                         in1=block_of(x1, tile), op0=ALU.mult, op1=ALU.add).then_inc(x1_done, 1)

            def stats_second(i):
                dve.wait_ge(x1_done, i + E)
                dve.bn_stats(bn2[:, :], block_of(x1, i)).then_inc(bn2_done, 1)
                dve.wait_ge(bn2_done, i + 1)
                if not isinstance(i, int) or i > 0:
                    dve.wait_ge(nmr2_done, i)

            def var_second(i):
                dve.bn_aggr(mv2[:, :], bn2[:, :]).then_inc(mv2_done, 1)
                dve.wait_ge(mv2_done, i + 1)
                dve.tensor_scalar(var2[:, :], mv2[:, 1:2], EPS, None, ALU.add).then_inc(var2_done, 1)

            def shift_second(i):
                dve.wait_ge(rstd2_done, i + 1)
                if not isinstance(i, int) or i > 0:
                    dve.wait_ge(h2_done, i)
                dve.scalar_tensor_tensor(out=nmr2[:, :], in0=mv2[:, 0:1], scalar=-1.0, in1=rstd2[:, :],
                                         op0=ALU.mult, op1=ALU.mult).then_inc(nmr2_done, 1)

            def max_second(i):
                dve.wait_ge(h2_done, i + 1)
                dve.tensor_reduce(rmax[:, bass.ds(i, 1)], block_of(h2, i), AX.X, ALU.max, apply_absolute_value=True)\
                    .then_inc(rmax_done, 1)

            def masks():
                routed(dve.scalar_tensor_tensor(out=job_slot[:, :], in0=job_e[:, :], scalar=-float(P),
                                                in1=iota_slot[:, :], op0=ALU.mult, op1=ALU.add))
                routed(dve.tensor_scalar(slot_e[:, :], job_slot[:, :], start[:, 1:2], None, ALU.is_ge))
                for e in range(2, E):
                    routed(dve.scalar_tensor_tensor(out=slot_e[:, :], in0=job_slot[:, :], scalar=start[:, e:e + 1],
                                                    in1=slot_e[:, :], op0=ALU.is_ge, op1=ALU.add))
                routed(dve.tensor_tensor(mask[:, :], slot_e[:, :], job_e[:, :], ALU.is_equal))
                dve.wait_ge(tanh_done, 1)
                routed(dve.tensor_scalar(mask[:, :], mask[:, :], tg[:, 0:1], None, ALU.mult))
                routed(dve.tensor_tensor(job_of[:, :, :], job_is[:, :, :],
                                         mask[:, :].unsqueeze(1).to_broadcast([P, E, JOBS]), ALU.mult))
                job_tables(0, ((job_mul, job_of, INV_Y),))
                job_tables(1)

            def job(j):
                fixed = isinstance(j, int)
                if not fixed or 0 < j < TILES - 2:
                    stats_first(j + 2)
                if not fixed or j < JOBS:
                    z_of(j)
                if fixed and j == 0:
                    masks()
                if fixed and 1 <= j and j + 1 < E:
                    w_scaling(j + 1)
                if not fixed or 0 < j < TILES - 2:
                    var_first(j + 2)
                if not fixed or j + 1 < TILES:
                    hT_low(j + 1)
                if fixed and j == 0:
                    w_low(1, range(2, K))
                if fixed and 1 <= j and j + 1 < E:
                    job_tables(j + 1)
                    w_low(j + 1, range(2))
                if not fixed or j > E:
                    shift_second(j - E - 1)
                if not fixed or j > E + 1:
                    max_second(j - E - 2)
                if not fixed or 1 <= j <= JOBS:
                    add_y(j - 1)
                if not fixed or j + 2 < TILES:
                    shift_first(j + 2)
                if fixed and 1 <= j and j + 1 < E:
                    w_low(j + 1, range(2, K))
                if not fixed or E <= j < TILES + E:
                    stats_second(j - E)
                if not fixed or j < JOBS:
                    zT_low(j)
                if not fixed or E <= j < TILES + E:
                    var_second(j - E)

            w_low(0, [0])
            stats_first(0)
            var_first(0)
            w_low(0, [1])
            shift_first(0)
            w_low(0, [2])
            stats_first(1)
            w_low(0, [3])
            var_first(1)
            w_scaling(1)
            shift_first(1)
            hT_low(0)
            stats_first(2)
            w_low(1, range(1))
            var_first(2)
            w_low(1, range(1, 2))
            for j in range(E + 2):
                job(j)
            for i in range(E + 4, TILES):
                dve.wait_ge(x_gathered[i], 16)
            with dve.Fori(E + 2, TILES - 2) as j:
                job(j)
            for j in range(TILES - 2, TILES + E + 1):
                job(j)
                if j == TILES - 2:
                    dve.wait_ge(wf_loaded, 16)
                    dve.tensor_reduce(wf_max[:, 0:1], wf[:, :], AX.X, ALU.max, apply_absolute_value=True)\
                        .then_inc(wf_step, 1)
                    dve.wait_ge(wf_step, 1)
                    dve.tensor_scalar(diag[:, :], ident[:, :], wf_max[:, 0:1], None, ALU.mult).then_inc(wf_step, 1)
                if j == TILES - 1:
                    dve.wait_ge(wf_max_done, 1)
                    routed(dve.tensor_reduce(wf_max[:, 1:2], m_ps[:, 0:P], AX.X, ALU.max))
                    routed(dve.tensor_scalar(wf_scale[:, :], wf_max[:, 1:2], 1.0 / E4M3_MAX, 1e-12, ALU.mult, ALU.max))
                    dve.reciprocal(wf_inv[:, :], wf_scale[:, :]).then_inc(wf_scaled, 1)
                if j == TILES:
                    dve.wait_ge(wfv_done, 1)
                    dve.tensor_scalar(wf_e[:, :].bitcast(I16), wf_v[:, :].bitcast(I16)[:, 1::2], EXP_MASK >> 16, None,
                                      ALU.bitwise_and).then_inc(wfe_done, 1)
                    dve.wait_ge(wfe_done, 1)
                    dve.tensor_scalar(wf_m[:, :], wf_e[:, :], 2.0 ** -6, 1.5 * 2.0 ** 20, ALU.max, ALU.mult)\
                        .then_inc(wfm_done, 1)
                if j == JOBS - 2:
                    cols = slice(K // 2 * D, K * D)
                    dve.wait_ge(wfm_done, 1)
                    dve.tensor_tensor(wf_v[:, cols], wf_v[:, cols], wf_m[:, cols], ALU.add).then_inc(wfs_done, 1)
                    dve.wait_ge(wfs_done, 1)
                    dve.tensor_tensor(wf_q[:, cols], wf_v[:, cols], wf_m[:, cols], ALU.subtract).then_inc(wfs_done, 1)
            max_second(TILES - 1)
            dve.wait_ge(rmax_done, TILES)
            dve.tensor_reduce(xmax[:, 0:1], rmax[:, :], AX.X, ALU.max).then_inc(xm_step, 1)
            dve.wait_ge(xm_step, 1)
            dve.tensor_scalar(diag[:, :], ident[:, :], xmax[:, 0:1], None, ALU.mult).then_inc(xm_step, 1)
            dve.wait_ge(xmax_done, 1)
            dve.tensor_reduce(xmax[:, 1:2], m_ps[:, P:2 * P], AX.X, ALU.max).then_inc(xm_step, 1)
            dve.wait_ge(xm_step, 3)
            routed(dve.tensor_scalar(x_scale[:, :], xmax[:, 1:2], 1.0 / E4M3_MAX, 1e-12, ALU.mult, ALU.max))
            dve.reciprocal(x_inv[:, :], x_scale[:, :]).then_inc(xm_step, 1)
            dve.tensor_tensor(out_scale[:, :], x_scale[:, :], wf_scale[:, :], ALU.mult).then_inc(xm_step, 1)

            def exponents(i):
                b = i % NB
                dve.wait_ge(v_done, i + 1)
                if i >= NB:
                    dve.wait_ge(vm_done, i - NB + 1)
                dve.tensor_scalar(ve[:, b, :].bitcast(I16), v[:, b, :].bitcast(I16), EXP_MASK >> 16, None,
                                  ALU.bitwise_and).then_inc(ve_done, 1)

            def grid(i):
                b = i % NB
                dve.wait_ge(ve_done, i + 1)
                if i >= NB:
                    dve.wait_ge(q8_done[i - NB], 1)
                dve.tensor_scalar(vm[:, b, :], ve[:, b, :], 2.0 ** -6, 1.5 * 2.0 ** 20, ALU.max, ALU.mult)\
                    .then_inc(vm_done, 1)

            def shifted(i):
                b = i % NB
                dve.wait_ge(vm_done, i + 1)
                dve.scalar_tensor_tensor(out=vt[:, b, :], in0=block_of(h2, i), scalar=x_inv[:, :], in1=vm[:, b, :],
                                         op0=ALU.mult, op1=ALU.add).then_inc(vt_done, 1)

            def rounded(i):
                b = i % NB
                dve.wait_ge(vt_done, i + 1)
                if i >= NB:
                    dve.wait_ge(qT_done, i - NB + 1)
                dve.tensor_tensor(q8[:, b, :], vt[:, b, :], vm[:, b, :], ALU.subtract).then_inc(q8_done[i], 1)

            def finish(i):
                dve.wait_ge(y8_done, i + 1)
                dve.scalar_tensor_tensor(out=block_of(x1, i), in0=y8[:, i % NB, :], scalar=tg[:, 1:2],
                                         in1=block_of(x1, i), op0=ALU.mult, op1=ALU.add).then_inc(out_done, 1)

            OUT_BEHIND = 3
            exponents(0)
            grid(0)
            for i in range(TILES + OUT_BEHIND):
                if i + 1 < TILES:
                    exponents(i + 1)
                if i < TILES:
                    shifted(i)
                if i + 1 < TILES:
                    grid(i + 1)
                if i >= OUT_BEHIND:
                    finish(i - OUT_BEHIND)
                if i < TILES and not on_pool(i):
                    rounded(i)


def kernel(**inputs):
    import numpy as _np
    import concourse.bacc as _bacc
    from concourse import mybir as _mybir
    from concourse.bass_utils import run_bass_kernel_spmd as _run

    nc = _bacc.Bacc("TRN2", target_bir_lowering=False, num_devices=1)
    a = {k: _np.asarray(v) for k, v in inputs.items()}
    B, S, D = a["x"].shape
    arrays = {
        "in_x": _np.ascontiguousarray(a["x"].reshape(B * S, D)),
        "in_ids": _np.ascontiguousarray(a["itok_BxS_13_99985"].reshape(P, B * S // P)),
        "in_ctx_t": _np.ascontiguousarray(a["ctx_2048"].transpose(0, 2, 1)),
        "in_g_x": _np.ascontiguousarray(a["g_xattn"].reshape(1)),
        "in_g_f": _np.ascontiguousarray(a["g_ffn"].reshape(1)),
        "in_wf_t": _np.ascontiguousarray(a["L0_ffn_weight"].T),
    }
    args = [nc.dram_tensor(n, v.shape, _mybir.dt.from_np(v.dtype), kind="ExternalInput").ap()
            for n, v in arrays.items()]
    args.append(nc.dram_tensor("out_0", (B * S, D), _mybir.dt.float32, kind="ExternalOutput").ap())
    gated_experts_kernel(nc, *args)
    r = _run(nc, [arrays], core_ids=[0])
    return r.results[0]["out_0"].reshape(B, S, D)
```

```python
from contextlib import ExitStack

import concourse.bass as bass
from concourse import mybir

ALU = mybir.AluOpType
ACT = mybir.ActivationFunctionType
AX = mybir.AxisListType
F32 = mybir.dt.float32
F16 = mybir.dt.float16
BF16 = mybir.dt.bfloat16
I32 = mybir.dt.int32
I16 = mybir.dt.int16

P = 128
VOCAB = 25000
EPS = 1e-5
H_SHIFT = 10
EXP_MASK = 0x7F800000
ONE = 1 << 23
BIAS = 127
ROW_MIN, ROW_MAX = 34, 104
NB = 8
NF = 4
E4M3_MAX = 448.0


def gated_experts_kernel(nc, x, ids, ctx_t, g_x, g_f, wf_t, out):
    T, D = x.shape
    E = ctx_t.shape[0]
    K = D // P
    TILES = T // P
    JOBS = TILES + E - 1
    C = ids.shape[1]
    PER = VOCAB // E
    C_DVE = 3 * C // 4
    assert ids.shape == (P, C) and P * C == T and D * 4 == 2048

    with ExitStack() as stack:
        def sb(name, shape, dt):
            return stack.enter_context(nc.sbuf_tensor(name, shape, dt))

        def psum(name, shape, dt):
            return stack.enter_context(nc.psum_tensor(name, shape, dt))

        def sem(name):
            return stack.enter_context(nc.semaphore(name))

        ident = sb("ident", [P, P], F32)
        ident_bf = sb("ident_bf", [P, P], BF16)
        below = sb("below", [P, P], F16)
        above = sb("above", [P, P], F16)
        ones_h = sb("ones_h", [P, P], F16)
        ones_bf = sb("ones_bf", [P, P], BF16)
        ones_f = sb("ones_f", [P, P], F32)
        scale_coef = sb("scale_coef", [P, 4], F32)
        scale_off = sb("scale_off", [P, 4], F32)
        iota_q = sb("iota_q", [P, P], F16)
        iota_tile = sb("iota_tile", [P, C, TILES], F32)
        token_no = sb("token_no", [P, C], F32)
        iota_job = sb("iota_job", [P, JOBS], F32)
        iota_slot = sb("iota_slot", [P, JOBS], F32)
        minus_half = sb("minus_half", [P, 1], F32)
        ids_s = sb("ids_s", [P, C], I32)
        reach = sb("reach", [P, E + 1, C], F32)
        member = sb("member", [P, E, C], F32)
        scan_one = sb("scan_one", [P, E * C], F32)
        count = sb("count", [P, E * C], F32)
        row_cum = sb("row_cum", [P, E + 1], F16)
        place = sb("place", [P, E, C], F32)
        slot_f = sb("slot_f", [P, C], F32)
        slot_i = sb("slot_i", [P, C], I32)
        q_i = sb("q_i", [P, C], I32)
        q_h = sb("q_h", [P, C], F16)
        q_neg = sb("q_neg", [P, C], F32)
        tile_i = sb("tile_i", [P, C], I32)
        tile_f = sb("tile_f", [P, C], F32)
        hit = sb("hit", [P, C, TILES], F32)
        pick = sb("pick", [P, C, TILES], F16)
        onehot = sb("onehot", [P, C, P], F16)
        token_of = sb("token_of", [P, TILES], I32)
        start = sb("start", [P, E], F32)
        start_i = sb("start_i", [P, E], I32)
        bound = sb("bound", [P, E], F32)
        job_e = sb("job_e", [P, JOBS], F32)
        job_slot = sb("job_slot", [P, JOBS], F32)
        slot_e = sb("slot_e", [P, JOBS], F32)
        mask = sb("mask", [P, JOBS], F32)
        job_expert_i = sb("job_expert_i", [1, JOBS], I32)
        job_tile_i = sb("job_tile_i", [1, JOBS], I32)
        g_s = sb("g_s", [P, 2], F32)
        tg = sb("tg", [P, 2], F32)
        row_sq = sb("row_sq", [P, E], F32)
        half_i = sb("half_i", [P, E], I32)
        half_f = sb("half_f", [P, E], F32)
        w_bits = sb("w_bits", [P, E, 4], I32)
        job_is = sb("job_is", [P, E, JOBS], F32)
        table_loaded = sb("table_loaded", [P, 1], F32)
        job_of = sb("job_of", [P, E, JOBS], F32)
        job_inv_a = sb("job_inv_a", [P, JOBS], F32)
        job_z_mul = sb("job_z_mul", [P, JOBS], F32)
        job_mul = sb("job_mul", [P, JOBS], F32)
        diag = sb("diag", [P, P], F32)
        wf_max = sb("wf_max", [P, 2], F32)
        wf_scale = sb("wf_scale", [P, 1], F32)
        wf_inv = sb("wf_inv", [P, 1], F32)
        rmax = sb("rmax", [P, TILES + 1], F32)
        ends = sb("ends", [P, 2], F32)
        xmax = sb("xmax", [P, 2], F32)
        x_scale = sb("x_scale", [P, 1], F32)
        x_inv = sb("x_inv", [P, 1], F32)
        out_scale = sb("out_scale", [P, 1], F32)
        x1 = sb("x1", [P, TILES * D], F32)
        w32 = sb("w32", [P, E * K * D], F32)
        h2 = w32
        w_hi = sb("w_hi", [P, E * K * D], F16)
        w_lo = sb("w_lo", [P, E * K * D], F16)
        hT_hi = sb("hT_hi", [P, TILES * D], F16)
        hT_lo = sb("hT_lo", [P, TILES * D], F16)
        h = sb("h", [P, D], F32)
        sg = sb("sg", [P, D], F32)
        az = sb("az", [P, D], F32)
        z = sb("z", [P, D], F32)
        zT_hi = sb("zT_hi", [P, D], F16)
        zT_lo = sb("zT_lo", [P, D], F16)
        bn1 = sb("bn1", [P, 6], F32)
        mv1 = sb("mv1", [P, 2], F32)
        var1 = sb("var1", [P, 1], F32)
        rstd1 = sb("rstd1", [P, 1], F32)
        nmr1 = sb("nmr1", [P, 1], F32)
        bn2 = sb("bn2", [P, 6], F32)
        mv2 = sb("mv2", [P, 2], F32)
        var2 = sb("var2", [P, 1], F32)
        rstd2 = sb("rstd2", [P, 1], F32)
        nmr2 = sb("nmr2", [P, 1], F32)
        wf = sb("wf", [P, K * D], BF16)
        wf_v = sb("wf_v", [P, K * D], F32)
        wf_e = sb("wf_e", [P, K * D], BF16)
        wf_m = sb("wf_m", [P, K * D], BF16)
        wf_q = sb("wf_q", [P, K * D], BF16)
        vt = w_hi[:, :].bitcast(F32)[:, 0:NB * D].rearrange("p (b d) -> p b d", b=NB)
        v_ve = hT_lo[:, :].bitcast(BF16).rearrange("p (b d) -> p b d", d=D)
        v, ve = v_ve[:, 0:NB, :], v_ve[:, NB:2 * NB, :]
        vm_q8 = hT_hi[:, :].bitcast(BF16).rearrange("p (b d) -> p b d", d=D)
        vm, q8 = vm_q8[:, 0:NB, :], vm_q8[:, NB:2 * NB, :]
        qT = sb("qT", [P, NF, D], BF16)
        y8 = sb("y8", [P, NB, D], BF16)

        a_ps = psum("a_ps", [P, D], F32)
        y_ps = psum("y_ps", [P, D], F32)
        hT_ps = psum("hT_ps", [P, D], F32)
        zT_ps = psum("zT_ps", [P, D], F32)
        r_ps = psum("r_ps", [P, 512], F32)
        c_ps = psum("c_ps", [P, 512], F32)
        n_ps = psum("n_ps", [P, 512], F32)
        m_ps = psum("m_ps", [P, 512], F32)
        f_ps = [a_ps, y_ps, hT_ps, zT_ps]
        qT_ps = [n_ps[:, :].bitcast(BF16), r_ps[:, :].bitcast(BF16), c_ps[:, :].bitcast(BF16)]
        NQ = len(qT_ps)
        base_ps = r_ps[:, 0:E]
        start_ps = c_ps[:, 64:64 + E + 1]
        sort_ps = c_ps[:, 0:TILES]

        ids_loaded, g_loaded, wf_loaded = sem("ids_loaded"), sem("g_loaded"), sem("wf_loaded")
        w_loaded = [sem(f"w_loaded{e}") for e in range(E)]
        x_gathered = [sem(f"x_gathered{i}") for i in range(TILES)]
        stored = sem("stored")
        pool_const, pool_fill = sem("pool_const"), sem("pool_fill")
        route = sem("route")
        sums_done, sort_done = sem("sums_done"), sem("sort_done")
        hit_done, pick_done = sem("hit_done"), sem("pick_done")
        q_ready, distance_done, onehot_done = sem("q_ready"), sem("distance_done"), sem("onehot_done")
        tokens_ready, jobs_ready = sem("tokens_ready"), sem("jobs_ready")
        tanh_done = sem("tanh_done")
        last_squares = sem("last_squares")
        squares_done, norms_done, norms_read = sem("squares_done"), sem("norms_done"), sem("norms_read")
        w_scales, job_scales, job_factors = sem("w_scales"), sem("job_scales"), sem("job_factors")
        wfs_done = sem("wfs_done")
        wf_step, wf_max_done, wf_scaled = sem("wf_step"), sem("wf_max_done"), sem("wf_scaled")
        nmr1_done, nmr2_done = sem("nmr1_done"), sem("nmr2_done")
        w_hi_done, w_lo_done = sem("w_hi_done"), sem("w_lo_done")
        bn1_done, mv1_done, var1_done, rstd1_done = sem("bn1_done"), sem("mv1_done"), sem("var1_done"), sem("rstd1_done")
        bn2_done, mv2_done, var2_done, rstd2_done = sem("bn2_done"), sem("mv2_done"), sem("var2_done"), sem("rstd2_done")
        h_done, hT_done = sem("h_done"), sem("hT_done")
        hT_hi_done, hT_lo_done = sem("hT_hi_done"), sem("hT_lo_done")
        a_done, az_done, silu_done, z_done, zT_done = sem("a_done"), sem("az_done"), sem("silu_done"), sem("z_done"), sem("zT_done")
        zT_hi_done, zT_lo_done, y_done, x1_done = sem("zT_hi_done"), sem("zT_lo_done"), sem("y_done"), sem("x1_done")
        h2_done, rmax_done = sem("h2_done"), sem("rmax_done")
        wfv_done, wfe_done, wfm_done, wft_done, wfq_done = (sem("wfv_done"), sem("wfe_done"), sem("wfm_done"),
                                                            sem("wft_done"), sem("wfq_done"))
        xm_step, xmax_done = sem("xm_step"), sem("xmax_done")
        v_done, ve_done, vm_done, vt_done = sem("v_done"), sem("ve_done"), sem("vm_done"), sem("vt_done")
        q8_done = [sem(f"q8_done{i}") for i in range(TILES)]
        qT_done, qT_copied, f_done, y8_done, out_done = (sem("qT_done"), sem("qT_copied"), sem("f_done"),
                                                         sem("y8_done"), sem("out_done"))

        M_OFF = 64 - BIAS
        SCALES = [(-1, BIAS + 15 - M_OFF),
                  (1, BIAS - 15 - H_SHIFT + M_OFF),
                  (-1, BIAS - 15 - H_SHIFT + 5 - M_OFF),
                  (3, BIAS - 15 - 5 + 3 * M_OFF)]
        S_W, INV_A, Z_MUL, INV_Y = range(4)

        def z_on_pool(j):
            return not isinstance(j, int) or 0 < j < TILES

        def w_scale(e, n):
            return w_bits[:, e, n:n + 1].bitcast(F32)

        def chunk(t, i, k):
            return t[:, bass.ds(i * D + k * P, P)]

        def block_of(t, i):
            return t[:, bass.ds(i * D, D)]

        def w_block(t, e, k):
            return t[:, bass.ds(e * (K * D) + k * D, D)]

        STORE_LAG = 5

        def on_pool(i):
            return i % 4 != 0 and i < TILES - 1

        block = stack.enter_context(nc.Block())

        @block.sync
        def _(sp):
            sp.dma_start(ids_s[:, :], ids).then_inc(ids_loaded, 16)
            for e in range(E):
                if e == 2:
                    sp.wait_ge(x_gathered[1], 16)
                sp.dma_start(w32[:, e * K * D:(e + 1) * K * D].rearrange("p (k f) -> p k f", k=K),
                             ctx_t[e].rearrange("(k p) f -> p k f", p=P)).then_inc(w_loaded[e], 16)
            sp.dma_start(wf[:, :].rearrange("p (k f) -> p k f", k=K),
                         wf_t.rearrange("(k p) f -> p k f", p=P)).then_inc(wf_loaded, 16)

        @block.gpsimd
        def _(pool):
            pool.memset(reach[:, 0, :], 1.0).then_inc(pool_fill, 1)
            pool.memset(reach[:, E, :], 0.0).then_inc(pool_fill, 1)
            pool.memset(scan_one[:, :], 1.0).then_inc(pool_fill, 1)
            pool.memset(row_cum[:, 0:1], 0.0).then_inc(pool_fill, 1)
            pool.memset(ident[:, :], 0.0).then_inc(pool_fill, 1)
            pool.memset(below[:, :], 1.0).then_inc(pool_fill, 1)
            pool.memset(above[:, :], 1.0).then_inc(pool_fill, 1)
            pool.memset(ones_h[:, :], 1.0).then_inc(pool_fill, 1)
            pool.wait_ge(pool_fill, 8)
            pool.affine_select(out=below[:, :], in_=below[:, :], compare_op=ALU.is_gt, fill=0.0, base=0,
                               pattern=[[1, P]], channel_multiplier=-1).then_inc(pool_const, 1)
            pool.affine_select(out=above[:, :], in_=above[:, :], compare_op=ALU.is_gt, fill=0.0, base=0,
                               pattern=[[-1, P]], channel_multiplier=1).then_inc(pool_const, 1)
            pool.iota(iota_q[:, :], [[1, P]], base=0, channel_multiplier=0,
                      allow_small_or_imprecise_dtypes=True).then_inc(pool_const, 1)
            pool.iota(token_no[:, :], [[1, C]], base=0, channel_multiplier=C,
                      allow_small_or_imprecise_dtypes=True).then_inc(pool_const, 1)
            pool.iota(iota_tile[:, :, :], [[0, C], [1, TILES]], base=0, channel_multiplier=0,
                      allow_small_or_imprecise_dtypes=True).then_inc(pool_const, 1)
            pool.iota(iota_job[:, :], [[1, JOBS]], base=0, channel_multiplier=0,
                      allow_small_or_imprecise_dtypes=True).then_inc(pool_const, 1)
            pool.iota(iota_slot[:, :], [[P, JOBS]], base=0, channel_multiplier=1,
                      allow_small_or_imprecise_dtypes=True).then_inc(pool_const, 1)
            pool.affine_select(out=ident[:, :], in_=ident[:, :], compare_op=ALU.not_equal, fill=1.0, base=0,
                               pattern=[[-1, P]], channel_multiplier=1).then_inc(pool_const, 1)
            pool.memset(minus_half[:, :], -0.5).then_inc(pool_const, 1)
            pool.memset(ones_bf[:, :], 1.0).then_inc(pool_const, 1)
            for n, (coef, off) in enumerate(SCALES):
                pool.memset(scale_coef[:, n:n + 1], float(coef))
                ins = pool.memset(scale_off[:, n:n + 1], float(off * ONE))
            ins.then_inc(pool_const, 1)
            pool.memset(ones_f[:, :], 1.0).then_inc(pool_const, 1)
            pool.wait_ge(pool_const, 12)
            pool.tensor_copy(ident_bf[:, :], ident[:, :]).then_inc(pool_const, 1)

            def gather(i):
                pool.indirect_dma_start(block_of(x1, i), None, x,
                                        bass.IndirectOffsetOnAxis(ap=token_of[:, i:i + 1], axis=0),
                                        bounds_check=T - 1).then_inc(x_gathered[i], 16)

            def rstd_first(i):
                pool.wait_ge(var1_done, i + 1)
                if not isinstance(i, int) or i > 0:
                    pool.wait_ge(h_done, i)
                    pool.wait_ge(nmr1_done, i)
                pool.tensor_tensor(rstd1[:, :], var1[:, :], minus_half[:, :], ALU.pow)\
                    .then_inc(rstd1_done, 1)

            def rstd_second(i):
                pool.wait_ge(var2_done, i + 1)
                if not isinstance(i, int) or i > 0:
                    pool.wait_ge(h2_done, i)
                    pool.wait_ge(nmr2_done, i)
                pool.tensor_tensor(rstd2[:, :], var2[:, :], minus_half[:, :], ALU.pow)\
                    .then_inc(rstd2_done, 1)

            def store_tile(i):
                pool.wait_ge(out_done, i + 1)
                pool.indirect_dma_start(out, bass.IndirectOffsetOnAxis(ap=token_of[:, i:i + 1], axis=0),
                                        block_of(x1, i), None, bounds_check=T - 1).then_inc(stored, 16)

            def z_of(j):
                pool.wait_ge(silu_done, j + 1)
                pool.wait_ge(az_done, j)
                pool.wait_ge(zT_done, j)
                pool.tensor_tensor(z[:, :], az[:, :], sg[:, :], ALU.mult).then_inc(z_done, 1)

            def job(j):
                if z_on_pool(j):
                    z_of(j)
                if isinstance(j, int) and JOBS - 2 <= j < JOBS:
                    k = j - JOBS + 2
                    cols = slice(k * D, (k + 1) * D)
                    pool.wait_ge(wfm_done, 1)
                    pool.tensor_tensor(wf_v[:, cols], wf_v[:, cols], wf_m[:, cols], ALU.add).then_inc(wft_done, 1)
                    pool.wait_ge(wft_done, k + 1)
                    pool.tensor_tensor(wf_q[:, cols], wf_v[:, cols], wf_m[:, cols], ALU.subtract).then_inc(wfq_done, 1)
                if not isinstance(j, int) or j + 2 < TILES:
                    rstd_first(j + 2)
                if not isinstance(j, int) or E <= j:
                    rstd_second(j - E)

            pool.wait_ge(hit_done, 1)
            pool.tensor_tensor(pick[:, :, :], hit[:, :, :], token_no[:, :].unsqueeze(2).to_broadcast([P, C, TILES]),
                               ALU.mult).then_inc(pick_done, 1)
            pool.wait_ge(tokens_ready, 1)
            after_gather = {4: 0, 7: 1, 11: 2}
            for i in range(TILES):
                gather(i)
                if i in after_gather:
                    rstd_first(after_gather[i])

            def last_square(k):
                pool.wait_ge(w_loaded[E - 1], 16)
                pool.tensor_tensor(w_block(w_lo, E - 1, k).bitcast(BF16), w_block(w32, E - 1, k),
                                   w_block(w32, E - 1, k), ALU.mult).then_inc(last_squares, 1)

            last_square(0)
            job(1)
            for k in range(1, K):
                last_square(k)
            for j in range(2, E + 1):
                job(j)
            with pool.Fori(E + 1, TILES - 2) as j:
                job(j)
            for j in range(TILES - 2, TILES + E):
                job(j)
            for i in range(TILES):
                if on_pool(i):
                    pool.wait_ge(vt_done, i + 1)
                    if i >= NB:
                        pool.wait_ge(qT_done, i - NB + 1)
                    pool.tensor_tensor(q8[:, i % NB, :], vt[:, i % NB, :], vm[:, i % NB, :], ALU.subtract)\
                        .then_inc(q8_done[i], 1)
                if i >= STORE_LAG:
                    store_tile(i - STORE_LAG)
            for i in range(TILES - STORE_LAG, TILES):
                store_tile(i)
            pool.wait_ge(stored, 16 * TILES)

        @block.tensor
        def _(pe):
            pe.wait_ge(pool_const, 2)
            pe.wait_ge(route, 4)
            pe.matmul(base_ps, above[:, :], row_cum[:, 0:E], start=True, stop=False)
            pe.matmul(base_ps, below[:, :], row_cum[:, 1:E + 1], start=False, stop=True).then_inc(sums_done, 1)
            pe.matmul(start_ps, ones_h[:, :], row_cum[:, :], start=True, stop=True).then_inc(sums_done, 1)

            def row_norms(e, k):
                if k == 0 and e > 0:
                    pe.wait_ge(norms_read, e)
                if e < E - 1:
                    pe.wait_ge(squares_done, K * e + k + 1)
                else:
                    pe.wait_ge(last_squares, k + 1)
                mm = pe.matmul(n_ps[:, :], ones_bf[:, :], w_block(w_lo, e, k).bitcast(BF16), start=(k == 0),
                               stop=(k == K - 1))
                if k == K - 1:
                    mm.then_inc(norms_done, 1)

            pe.wait_ge(pool_const, 10)
            pe.wait_ge(pick_done, 1)
            for c in range(C):
                if c % 4 == 0:
                    pe.wait_ge(onehot_done, c + 4)
                mm = pe.matmul(sort_ps, onehot[:, c, :], pick[:, c, :], start=(c == 0), stop=(c == C - 1))
            mm.then_inc(sort_done, 1)
            for k in range(K):
                row_norms(0, k)

            def transpose_h(i):
                pe.wait_ge(h_done, i + 1)
                for k in range(K):
                    mm = pe.transpose(hT_ps[:, k * P:(k + 1) * P], h[:, k * P:(k + 1) * P], ident[:, :])
                mm.then_inc(hT_done, 1)

            def product(ps, lhs_hi, lhs_lo, expert, lo_ready, first=None):
                for k in range(K):
                    if first is not None:
                        pe.wait_ge(w_hi_done, K * first + k + 1)
                    pe.matmul(ps, lhs_hi(k), w_block(w_hi, expert, k), start=(k == 0), stop=False)
                if first is not None:
                    lo_ready()
                    for k in range(K):
                        pe.matmul(ps, lhs_lo(k), w_block(w_hi, expert, k), start=False, stop=False)
                for k in range(K):
                    if first is not None:
                        pe.wait_ge(w_lo_done, K * first + k + 1)
                    mm = pe.matmul(ps, lhs_hi(k), w_block(w_lo, expert, k), start=False,
                                   stop=(first is not None and k == K - 1))
                if first is None:
                    lo_ready()
                    for k in range(K):
                        mm = pe.matmul(ps, lhs_lo(k), w_block(w_hi, expert, k), start=False, stop=(k == K - 1))
                return mm

            def up(j, tile, expert):
                loading = not isinstance(j, int) or j < TILES
                if loading:
                    pe.wait_ge(hT_hi_done, j + 1)

                def lo_ready():
                    if loading:
                        pe.wait_ge(hT_lo_done, j + 1)

                product(a_ps[:, :], lambda k: chunk(hT_hi, tile, k), lambda k: chunk(hT_lo, tile, k), expert,
                        lo_ready, j if isinstance(j, int) and j < E else None).then_inc(a_done, 1)

            def down(j, expert):
                pe.wait_ge(zT_hi_done, j + 1)
                if not isinstance(j, int) or j > 0:
                    pe.wait_ge(x1_done, j)
                product(y_ps[:, :], lambda k: zT_hi[:, k * P:(k + 1) * P], lambda k: zT_lo[:, k * P:(k + 1) * P],
                        expert, lambda: pe.wait_ge(zT_lo_done, j + 1)).then_inc(y_done, 1)

            def transpose_z(j):
                pe.wait_ge(z_done, j + 1)
                for k in range(K):
                    mm = pe.transpose(zT_ps[:, k * P:(k + 1) * P], z[:, k * P:(k + 1) * P], ident[:, :])
                mm.then_inc(zT_done, 1)

            def expert_of(j):
                return pe.value_load(job_expert_i[0:1, bass.ds(j, 1)], min_val=0, max_val=E - 1)

            def tile_of(j):
                return pe.value_load(job_tile_i[0:1, bass.ds(j, 1)], min_val=0, max_val=TILES - 1)

            def job(j):
                if not isinstance(j, int) or j > 0:
                    expert_before = expert_of(j - 1)
                if isinstance(j, int) and j == 2:
                    for k in range(K):
                        row_norms(3, k)
                if not isinstance(j, int) or j + 1 < TILES:
                    transpose_h(j + 1)
                if isinstance(j, int) and j == 1:
                    for k in range(K):
                        row_norms(2, k)
                if not isinstance(j, int) or j > 0:
                    down(j - 1, expert_before)
                if not isinstance(j, int) or j + 1 < JOBS:
                    next_tile, next_expert = tile_of(j + 1), expert_of(j + 1)
                transpose_z(j)
                if not isinstance(j, int) or j + 1 < JOBS:
                    up(j + 1, next_tile, next_expert)

            pe.wait_ge(jobs_ready, 2)
            first_tile, first_expert = tile_of(0), expert_of(0)
            row_norms(1, 0)
            transpose_h(0)
            for k in range(1, K):
                row_norms(1, k)
            up(0, first_tile, first_expert)
            for j in range(E):
                job(j)
            with pe.Fori(E, TILES - 2, 2) as j:
                job(j)
                job(j + 1)
            for j in range(TILES - 2, JOBS):
                job(j)
                if j == TILES - 1:
                    pe.wait_ge(pool_const, 12)
                    pe.wait_ge(wf_step, 2)
                    pe.matmul(m_ps[:, 0:P], ones_f[:, :], diag[:, :], start=True, stop=True).then_inc(wf_max_done, 1)
            down(JOBS - 1, expert_of(JOBS - 1))

            pe.wait_ge(xm_step, 2)
            pe.matmul(m_ps[:, P:2 * P], ones_f[:, :], diag[:, :], start=True, stop=True).then_inc(xmax_done, 1)

            def transpose_q(i):
                pe.wait_ge(q8_done[i], 1)
                if i >= NQ:
                    pe.wait_ge(qT_copied, i - NQ + 1)
                for k in range(K):
                    mm = pe.transpose(qT_ps[i % NQ][:, k * P:(k + 1) * P], q8[:, i % NB, k * P:(k + 1) * P],
                                      ident_bf[:, :])
                mm.then_inc(qT_done, 1)

            pe.wait_ge(pool_const, 13)
            pe.wait_ge(wfq_done, K // 2)
            pe.wait_ge(wfs_done, 1 + K // 2)
            transpose_q(0)
            for i in range(TILES):
                if i + 1 < TILES:
                    transpose_q(i + 1)
                pe.wait_ge(qT_copied, i + 1)
                if i >= NF:
                    pe.wait_ge(y8_done, i - NF + 1)
                for k in range(K):
                    mm = pe.matmul(f_ps[i % NF][:, :], qT[:, i % NF, k * P:(k + 1) * P], wf_q[:, k * D:(k + 1) * D],
                                   start=(k == 0), stop=(k == K - 1))
                mm.then_inc(f_done, 1)

        @block.scalar
        def _(act):
            act.dma_start(g_s[:, 0:1], g_x.partition_broadcast(P)).then_inc(g_loaded, 16)
            act.dma_start(g_s[:, 1:2], g_f.partition_broadcast(P)).then_inc(g_loaded, 16)
            act.wait_ge(pool_fill, 3)
            act.activation(table_loaded[:, :], scan_one[:, 0:1], ACT.Silu)

            def hT_high(i):
                act.wait_ge(hT_done, i + 1)
                act.activation(block_of(hT_hi, i), hT_ps[:, :], ACT.Copy).then_inc(hT_hi_done, 1)

            def squares(e, chunks=range(K)):
                act.wait_ge(w_loaded[e], 16)
                for k in chunks:
                    act.activation(w_block(w_lo, e, k).bitcast(BF16), w_block(w32, e, k), ACT.Square)\
                        .then_inc(squares_done, 1)

            def w_high(e):
                act.wait_ge(w_scales, e + 1)
                for k in range(K):
                    act.activation(w_block(w_hi, e, k), w_block(w32, e, k), ACT.Copy, scale=w_scale(e, S_W))\
                        .then_inc(w_hi_done, 1)

            def norm_first(i):
                act.wait_ge(nmr1_done, i + 1)
                if not isinstance(i, int) or i > 0:
                    act.wait_ge(hT_done, i)
                act.activation(h[:, :], block_of(x1, i), ACT.Identity, bias=nmr1[:, :], scale=rstd1[:, :])\
                    .then_inc(h_done, 1)

            def norm_second(i):
                act.wait_ge(nmr2_done, i + 1)
                act.activation(block_of(h2, i), block_of(x1, i), ACT.Identity, bias=nmr2[:, :], scale=rstd2[:, :])\
                    .then_inc(h2_done, 1)

            def silu(j):
                act.wait_ge(a_done, j + 1)
                if isinstance(j, int) and j < E:
                    act.wait_ge(job_scales, 2 * (j + 1))
                if not isinstance(j, int) or j > 0:
                    act.wait_ge(z_done, j)
                act.activation(sg[:, :], a_ps[:, :], ACT.Silu, scale=job_inv_a[:, bass.ds(j, 1)]).then_inc(silu_done, 1)
                if z_on_pool(j):
                    act.activation(az[:, :], a_ps[:, :], ACT.Copy, scale=job_z_mul[:, bass.ds(j, 1)])\
                        .then_inc(az_done, 1)

            def zT_high(j):
                act.wait_ge(zT_done, j + 1)
                if not isinstance(j, int) or j > 0:
                    act.wait_ge(y_done, j)
                act.activation(zT_hi[:, :], zT_ps[:, :], ACT.Copy).then_inc(zT_hi_done, 1)

            def job(j):
                fixed = isinstance(j, int)
                if not fixed or j < JOBS:
                    silu(j)
                if not fixed or j + 1 < TILES:
                    hT_high(j + 1)
                if fixed and j == 0:
                    squares(2, range(2))
                if fixed and 1 <= j and j + 1 < E:
                    w_high(j + 1)
                if not fixed or j > E:
                    norm_second(j - E - 1)
                if not fixed or j < JOBS:
                    zT_high(j)
                if not fixed or j + 2 < TILES:
                    norm_first(j + 2)
                if fixed and j == 0:
                    squares(2, range(2, K))

            act.wait_ge(pool_const, 3)
            act.wait_ge(q_ready, 1)
            for c in range(C_DVE, C):
                act.activation(onehot[:, c, :], iota_q[:, :], ACT.Identity, bias=q_neg[:, c:c + 1])\
                    .then_inc(distance_done, 1)
            squares(0)
            act.wait_ge(g_loaded, 32)
            act.activation(tg[:, :], g_s[:, :], ACT.Tanh).then_inc(tanh_done, 1)
            w_high(0)
            squares(1, range(1))
            norm_first(0)
            squares(1, range(1, K))
            hT_high(0)
            norm_first(1)
            w_high(1)
            for j in range(E + 1):
                job(j)
                if j == E:
                    act.wait_ge(w_lo_done, K * E)
            with act.Fori(E + 1, TILES - 2) as j:
                job(j)
            for j in range(TILES - 2, TILES + E + 1):
                job(j)
                if j == TILES:
                    act.wait_ge(wf_scaled, 1)
                    act.activation(wf_v[:, :], wf[:, :], ACT.Copy, scale=wf_inv[:, :]).then_inc(wfv_done, 1)

            def scaled(i):
                if i >= NB:
                    act.wait_ge(ve_done, i - NB + 1)
                act.activation(v[:, i % NB, :], block_of(h2, i), ACT.Copy, scale=x_inv[:, :]).then_inc(v_done, 1)

            def copy_qT(i):
                act.wait_ge(qT_done, i + 1)
                if i >= NF:
                    act.wait_ge(f_done, i - NF + 1)
                act.activation(qT[:, i % NF, :], qT_ps[i % NQ][:, 0:D], ACT.Copy).then_inc(qT_copied, 1)

            def to_bf16(i):
                act.wait_ge(f_done, i + 1)
                if i >= NB:
                    act.wait_ge(out_done, i - NB + 1)
                act.activation(y8[:, i % NB, :], f_ps[i % NF][:, :], ACT.Copy, scale=out_scale[:, :])\
                    .then_inc(y8_done, 1)

            act.wait_ge(xm_step, 5)
            V_AHEAD, Y_BEHIND = 7, 1
            for i in range(V_AHEAD):
                scaled(i)
            for i in range(TILES + Y_BEHIND):
                if i < TILES:
                    copy_qT(i)
                if i + V_AHEAD < TILES:
                    scaled(i + V_AHEAD)
                if i >= Y_BEHIND:
                    to_bf16(i - Y_BEHIND)

        @block.vector
        def _(dve):
            step = [0]

            def routed(ins):
                step[0] += 1
                ins.then_inc(route, 1)
                dve.wait_ge(route, step[0])

            dve.wait_ge(ids_loaded, 16)
            dve.wait_ge(pool_fill, 4)
            for e in range(1, E):
                ins = dve.tensor_scalar(reach[:, e, :], ids_s[:, :], float(e * PER), None, ALU.is_ge)
            routed(ins)
            routed(dve.tensor_tensor(member[:, :, :], reach[:, 0:E, :], reach[:, 1:E + 1, :], ALU.subtract))
            routed(dve.tensor_tensor_scan(count[:, :], scan_one[:, :], member[:, :, :].rearrange("p e c -> p (e c)"),
                                          0.0, ALU.mult, ALU.add))
            routed(dve.tensor_copy(row_cum[:, 1:E + 1], count[:, C - 1:E * C:C]))
            dve.wait_ge(sums_done, 1)
            routed(dve.tensor_tensor(place[:, :, :], count[:, :].rearrange("p (e c) -> p e c", e=E),
                                     base_ps.unsqueeze(2).to_broadcast([P, E, C]), ALU.add))
            routed(dve.tensor_tensor(place[:, :, :], place[:, :, :], member[:, :, :], ALU.mult))
            routed(dve.tensor_reduce(slot_f[:, :], place[:, :, :].rearrange("p e c -> p c e"), AX.X, ALU.add))
            routed(dve.tensor_scalar(slot_i[:, :], slot_f[:, :], -1.0, None, ALU.add))
            dve.tensor_scalar(q_i[:, :], slot_i[:, :], P - 1, None, ALU.bitwise_and)
            routed(dve.tensor_scalar(tile_i[:, :], slot_i[:, :], P.bit_length() - 1, None, ALU.logical_shift_right))
            dve.tensor_scalar(q_neg[:, :], q_i[:, :], -1.0, None, ALU.mult).then_inc(q_ready, 1)
            dve.tensor_copy(q_h[:, :], q_i[:, :])
            routed(dve.tensor_copy(tile_f[:, :], tile_i[:, :]))
            dve.wait_ge(pool_const, 5)
            dve.tensor_tensor(hit[:, :, :], iota_tile[:, :, :], tile_f[:, :].unsqueeze(2).to_broadcast([P, C, TILES]),
                              ALU.is_equal).then_inc(hit_done, 1)
            for c in range(0, C, 4):
                if c < C_DVE:
                    ins = dve.tensor_tensor(onehot[:, c:c + 4, :], iota_q[:, :].unsqueeze(1).to_broadcast([P, 4, P]),
                                            q_h[:, c:c + 4].unsqueeze(2).to_broadcast([P, 4, P]), ALU.is_equal)
                else:
                    dve.wait_ge(distance_done, c + 4 - C_DVE)
                    ins = dve.tensor_scalar(onehot[:, c:c + 4, :], onehot[:, c:c + 4, :], 0.0, None, ALU.is_equal)
                ins.then_inc(onehot_done, 4)
            dve.wait_ge(sort_done, 1)
            dve.tensor_copy(token_of[:, :], sort_ps).then_inc(tokens_ready, 1)

            def w_scaling(e):
                dve.wait_ge(norms_done, e + 1)
                dve.tensor_reduce(row_sq[:, e:e + 1], n_ps[:, :], AX.X, ALU.max).then_inc(norms_read, 1)
                dve.wait_ge(norms_read, e + 1)
                routed(dve.tensor_scalar(half_i[:, e:e + 1], row_sq[:, e:e + 1].bitcast(I32), 1, EXP_MASK,
                                         ALU.logical_shift_right, ALU.bitwise_and))
                routed(dve.tensor_scalar(half_f[:, e:e + 1], half_i[:, e:e + 1], float(ROW_MIN * ONE),
                                         float(ROW_MAX * ONE), ALU.max, ALU.min))
                if e == 0:
                    dve.wait_ge(pool_const, 11)
                dve.scalar_tensor_tensor(out=w_bits[:, e, :], in0=scale_coef[:, :], scalar=half_f[:, e:e + 1],
                                         in1=scale_off[:, :], op0=ALU.mult, op1=ALU.add).then_inc(w_scales, 1)
                dve.wait_ge(w_scales, e + 1)

            dve.wait_ge(sums_done, 2)
            dve.tensor_copy(start[:, :], start_ps[:, 0:E])
            routed(dve.tensor_copy(start_i[:, :], start_ps[:, 0:E]))
            routed(dve.tensor_scalar(start_i[:, :], start_i[:, :], P.bit_length() - 1, None, ALU.logical_shift_right))
            for e in range(1, E):
                ins = dve.tensor_scalar(bound[:, e:e + 1], start_i[:, e:e + 1], float(TILES - 1), float(e),
                                        ALU.min, ALU.add)
            routed(ins)
            dve.wait_ge(pool_const, 7)
            routed(dve.tensor_scalar(job_e[:, :], iota_job[:, :], bound[:, 1:2], None, ALU.is_ge))
            for e in range(2, E):
                routed(dve.scalar_tensor_tensor(out=job_e[:, :], in0=iota_job[:, :], scalar=bound[:, e:e + 1],
                                                in1=job_e[:, :], op0=ALU.is_ge, op1=ALU.add))
            dve.tensor_copy(job_expert_i[:, :], job_e[0:1, :]).then_inc(jobs_ready, 1)
            dve.tensor_tensor(job_tile_i[:, :], iota_job[0:1, :], job_e[0:1, :], ALU.subtract).then_inc(jobs_ready, 1)
            w_scaling(0)
            for e in range(E):
                ins = dve.tensor_scalar(job_is[:, e, :], job_e[:, :], float(e), None, ALU.is_equal)
            routed(ins)

            def add_expert(table, chosen, e, n):
                if e == 0:
                    return dve.tensor_scalar(table[:, :], chosen[:, 0, :], w_scale(0, n), None, ALU.mult)
                return dve.scalar_tensor_tensor(out=table[:, e:], in0=chosen[:, e, e:], scalar=w_scale(e, n),
                                                in1=table[:, e:], op0=ALU.mult, op1=ALU.add)

            def product_tables(e):
                if e > 0:
                    dve.wait_ge(job_scales, 2 * e)
                add_expert(job_inv_a, job_is, e, INV_A).then_inc(job_scales, 1)
                add_expert(job_z_mul, job_is, e, Z_MUL).then_inc(job_scales, 1)

            def result_table(e):
                if e > 0:
                    dve.wait_ge(job_factors, e)
                add_expert(job_mul, job_of, e, INV_Y).then_inc(job_factors, 1)

            product_tables(0)

            def w_low(e, chunks=range(K)):
                for k in chunks:
                    dve.wait_ge(w_hi_done, K * e + k + 1)
                    dve.scalar_tensor_tensor(out=w_block(w_lo, e, k), in0=w_block(w32, e, k), scalar=w_scale(e, S_W),
                                             in1=w_block(w_hi, e, k), op0=ALU.mult, op1=ALU.subtract)\
                        .then_inc(w_lo_done, 1)

            def stats_first(i):
                if isinstance(i, int):
                    dve.wait_ge(x_gathered[i], 16)
                dve.bn_stats(bn1[:, :], block_of(x1, i)).then_inc(bn1_done, 1)
                dve.wait_ge(bn1_done, i + 1)
                if not isinstance(i, int) or i > 0:
                    dve.wait_ge(nmr1_done, i)

            def var_first(i):
                dve.bn_aggr(mv1[:, :], bn1[:, :]).then_inc(mv1_done, 1)
                dve.wait_ge(mv1_done, i + 1)
                dve.tensor_scalar(var1[:, :], mv1[:, 1:2], EPS, 0.25 ** H_SHIFT, ALU.add, ALU.mult)\
                    .then_inc(var1_done, 1)

            def shift_first(i):
                dve.wait_ge(rstd1_done, i + 1)
                if not isinstance(i, int) or i > 0:
                    dve.wait_ge(h_done, i)
                dve.scalar_tensor_tensor(out=nmr1[:, :], in0=mv1[:, 0:1], scalar=-1.0, in1=rstd1[:, :],
                                         op0=ALU.mult, op1=ALU.mult).then_inc(nmr1_done, 1)

            def hT_low(i):
                dve.wait_ge(hT_hi_done, i + 1)
                dve.tensor_tensor(block_of(hT_lo, i), hT_ps[:, :], block_of(hT_hi, i), ALU.subtract)\
                    .then_inc(hT_lo_done, 1)

            def z_of(j):
                dve.wait_ge(silu_done, j + 1)
                if j > 0:
                    dve.wait_ge(zT_done, j)
                dve.scalar_tensor_tensor(out=z[:, :], in0=a_ps[:, :], scalar=job_z_mul[:, j:j + 1], in1=sg[:, :],
                                         op0=ALU.mult, op1=ALU.mult).then_inc(z_done, 1)

            def zT_low(j):
                dve.wait_ge(zT_hi_done, j + 1)
                dve.tensor_tensor(zT_lo[:, :], zT_ps[:, :], zT_hi[:, :], ALU.subtract).then_inc(zT_lo_done, 1)

            def add_y(j):
                tile = dve.value_load(job_tile_i[0:1, bass.ds(j, 1)], min_val=0, max_val=TILES - 1)
                dve.wait_ge(y_done, j + 1)
                if not isinstance(j, int) or j > 0:
                    dve.wait_ge(x1_done, j)
                dve.scalar_tensor_tensor(out=block_of(x1, tile), in0=y_ps[:, :], scalar=job_mul[:, bass.ds(j, 1)],
                                         in1=block_of(x1, tile), op0=ALU.mult, op1=ALU.add).then_inc(x1_done, 1)

            def stats_second(i):
                dve.wait_ge(x1_done, i + E)
                dve.bn_stats(bn2[:, :], block_of(x1, i)).then_inc(bn2_done, 1)
                dve.wait_ge(bn2_done, i + 1)
                if not isinstance(i, int) or i > 0:
                    dve.wait_ge(nmr2_done, i)

            def var_second(i):
                dve.bn_aggr(mv2[:, :], bn2[:, :]).then_inc(mv2_done, 1)
                dve.wait_ge(mv2_done, i + 1)
                dve.tensor_scalar(var2[:, :], mv2[:, 1:2], EPS, None, ALU.add).then_inc(var2_done, 1)

            def shift_second(i):
                dve.wait_ge(rstd2_done, i + 1)
                if not isinstance(i, int) or i > 0:
                    dve.wait_ge(h2_done, i)
                dve.scalar_tensor_tensor(out=nmr2[:, :], in0=mv2[:, 0:1], scalar=-1.0, in1=rstd2[:, :],
                                         op0=ALU.mult, op1=ALU.mult).then_inc(nmr2_done, 1)

            def max_second(i):
                dve.wait_ge(h2_done, i + 1)
                dve.tensor_reduce(rmax[:, bass.ds(i, 1)], block_of(h2, i), AX.X, ALU.max, apply_absolute_value=True)\
                    .then_inc(rmax_done, 1)

            def wf_rounded(k):
                cols = slice(k * D, (k + 1) * D)
                dve.wait_ge(wfs_done, 1)
                dve.tensor_tensor(wf_q[:, cols], wf_v[:, cols], wf_m[:, cols], ALU.subtract).then_inc(wfs_done, 1)

            def masks():
                routed(dve.scalar_tensor_tensor(out=job_slot[:, :], in0=job_e[:, :], scalar=-float(P),
                                                in1=iota_slot[:, :], op0=ALU.mult, op1=ALU.add))
                routed(dve.tensor_scalar(slot_e[:, :], job_slot[:, :], start[:, 1:2], None, ALU.is_ge))
                for e in range(2, E):
                    routed(dve.scalar_tensor_tensor(out=slot_e[:, :], in0=job_slot[:, :], scalar=start[:, e:e + 1],
                                                    in1=slot_e[:, :], op0=ALU.is_ge, op1=ALU.add))
                routed(dve.tensor_tensor(mask[:, :], slot_e[:, :], job_e[:, :], ALU.is_equal))
                dve.wait_ge(tanh_done, 1)
                routed(dve.tensor_scalar(mask[:, :], mask[:, :], tg[:, 0:1], None, ALU.mult))
                routed(dve.tensor_tensor(job_of[:, :, :], job_is[:, :, :],
                                         mask[:, :].unsqueeze(1).to_broadcast([P, E, JOBS]), ALU.mult))
                result_table(0)
                result_table(1)

            def job(j):
                fixed = isinstance(j, int)
                if not fixed or 0 < j < TILES - 2:
                    stats_first(j + 2)
                if fixed and j == TILES + E:
                    for n, op in enumerate([ALU.max, ALU.min]):
                        dve.tensor_reduce(ends[:, n:n + 1], block_of(x1, TILES - 1), AX.X, op).then_inc(rmax_done, 1)
                if not fixed or j > E:
                    shift_second(j - E - 1)
                if not fixed or 0 < j < TILES - 2:
                    var_first(j + 2)
                if fixed and j < JOBS and not z_on_pool(j):
                    z_of(j)
                if fixed and 1 <= j and j + 1 < E:
                    w_scaling(j + 1)
                    w_low(j + 1, [0])
                if not fixed or j > E + 1:
                    max_second(j - E - 2)
                if fixed and j == JOBS - 1:
                    for k in range(K // 2, K - 1):
                        wf_rounded(k)
                if not fixed or j + 1 < TILES:
                    hT_low(j + 1)
                if fixed and j == 0:
                    w_low(1, [3])
                    shift_first(2)
                    masks()
                if fixed and 1 <= j and j + 1 < E:
                    shift_first(j + 2)
                    w_low(j + 1, range(1, K))
                    product_tables(j + 1)
                    result_table(j + 1)
                if not fixed or 1 <= j <= JOBS:
                    add_y(j - 1)
                if not fixed or E - 1 <= j < TILES - 2:
                    shift_first(j + 2)
                if not fixed or E <= j < TILES + E:
                    stats_second(j - E)
                if not fixed or j < JOBS:
                    zT_low(j)
                if not fixed or E <= j < TILES + E:
                    var_second(j - E)

            w_low(0, [0])
            stats_first(0)
            var_first(0)
            w_low(0, [1])
            shift_first(0)
            w_low(0, [2])
            stats_first(1)
            w_low(0, [3])
            var_first(1)
            hT_low(0)
            shift_first(1)
            w_scaling(1)
            product_tables(1)
            stats_first(2)
            w_low(1, [0])
            var_first(2)
            w_low(1, [1, 2])
            for j in range(E + 2):
                job(j)
            for i in range(E + 4, TILES):
                dve.wait_ge(x_gathered[i], 16)
            with dve.Fori(E + 2, TILES - 2) as j:
                job(j)
            for j in range(TILES - 2, TILES + E + 1):
                job(j)
                if j == TILES - 2:
                    dve.wait_ge(wf_loaded, 16)
                    dve.tensor_reduce(wf_max[:, 0:1], wf[:, :], AX.X, ALU.max, apply_absolute_value=True)\
                        .then_inc(wf_step, 1)
                    dve.wait_ge(wf_step, 1)
                    dve.tensor_scalar(diag[:, :], ident[:, :], wf_max[:, 0:1], None, ALU.mult).then_inc(wf_step, 1)
                if j == TILES - 1:
                    dve.wait_ge(wf_max_done, 1)
                    routed(dve.tensor_reduce(wf_max[:, 1:2], m_ps[:, 0:P], AX.X, ALU.max))
                    routed(dve.tensor_scalar(wf_scale[:, :], wf_max[:, 1:2], 1.0 / E4M3_MAX, 1e-12, ALU.mult, ALU.max))
                    dve.reciprocal(wf_inv[:, :], wf_scale[:, :]).then_inc(wf_scaled, 1)
                if j == TILES:
                    dve.wait_ge(wfv_done, 1)
                    dve.tensor_scalar(wf_e[:, :].bitcast(I16), wf_v[:, :].bitcast(I16)[:, 1::2], EXP_MASK >> 16, None,
                                      ALU.bitwise_and).then_inc(wfe_done, 1)
                    dve.wait_ge(wfe_done, 1)
                    dve.tensor_scalar(wf_m[:, :], wf_e[:, :], 2.0 ** -6, 1.5 * 2.0 ** 20, ALU.max, ALU.mult)\
                        .then_inc(wfm_done, 1)
                if j == JOBS - 2:
                    cols = slice(K // 2 * D, K * D)
                    dve.wait_ge(wfm_done, 1)
                    dve.tensor_tensor(wf_v[:, cols], wf_v[:, cols], wf_m[:, cols], ALU.add).then_inc(wfs_done, 1)
                if j == JOBS - 1:
                    wf_rounded(K - 1)
            dve.wait_ge(nmr2_done, TILES)
            dve.wait_ge(rmax_done, TILES + 1)
            dve.tensor_scalar(rmax[:, TILES - 1:TILES + 1], ends[:, :], rstd2[:, :], nmr2[:, :], ALU.mult, ALU.add)\
                .then_inc(rmax_done, 1)
            dve.wait_ge(rmax_done, TILES + 2)
            dve.tensor_reduce(xmax[:, 0:1], rmax[:, :], AX.X, ALU.max, apply_absolute_value=True).then_inc(xm_step, 1)
            dve.wait_ge(xm_step, 1)
            dve.tensor_scalar(diag[:, :], ident[:, :], xmax[:, 0:1], None, ALU.mult).then_inc(xm_step, 1)
            dve.wait_ge(xmax_done, 1)
            dve.tensor_reduce(xmax[:, 1:2], m_ps[:, P:2 * P], AX.X, ALU.max).then_inc(xm_step, 1)
            dve.wait_ge(xm_step, 3)
            routed(dve.tensor_scalar(x_scale[:, :], xmax[:, 1:2], 1.0 / E4M3_MAX, 1e-12, ALU.mult, ALU.max))
            dve.reciprocal(x_inv[:, :], x_scale[:, :]).then_inc(xm_step, 1)
            dve.tensor_tensor(out_scale[:, :], x_scale[:, :], wf_scale[:, :], ALU.mult).then_inc(xm_step, 1)

            def exponents(i):
                b = i % NB
                dve.wait_ge(v_done, i + 1)
                if i >= NB:
                    dve.wait_ge(vm_done, i - NB + 1)
                dve.tensor_scalar(ve[:, b, :].bitcast(I16), v[:, b, :].bitcast(I16), EXP_MASK >> 16, None,
                                  ALU.bitwise_and).then_inc(ve_done, 1)

            def grid(i):
                b = i % NB
                dve.wait_ge(ve_done, i + 1)
                if i >= NB:
                    dve.wait_ge(q8_done[i - NB], 1)
                dve.tensor_scalar(vm[:, b, :], ve[:, b, :], 2.0 ** -6, 1.5 * 2.0 ** 20, ALU.max, ALU.mult)\
                    .then_inc(vm_done, 1)

            def shifted(i):
                b = i % NB
                dve.wait_ge(vm_done, i + 1)
                dve.scalar_tensor_tensor(out=vt[:, b, :], in0=block_of(h2, i), scalar=x_inv[:, :], in1=vm[:, b, :],
                                         op0=ALU.mult, op1=ALU.add).then_inc(vt_done, 1)

            def rounded(i):
                b = i % NB
                dve.wait_ge(vt_done, i + 1)
                if i >= NB:
                    dve.wait_ge(qT_done, i - NB + 1)
                dve.tensor_tensor(q8[:, b, :], vt[:, b, :], vm[:, b, :], ALU.subtract).then_inc(q8_done[i], 1)

            def finish(i):
                dve.wait_ge(y8_done, i + 1)
                dve.scalar_tensor_tensor(out=block_of(x1, i), in0=y8[:, i % NB, :], scalar=tg[:, 1:2],
                                         in1=block_of(x1, i), op0=ALU.mult, op1=ALU.add).then_inc(out_done, 1)

            OUT_BEHIND = 5
            exponents(0)
            grid(0)
            for i in range(TILES + OUT_BEHIND):
                if i + 1 < TILES:
                    exponents(i + 1)
                if i < TILES:
                    shifted(i)
                if i + 1 < TILES:
                    grid(i + 1)
                if i >= OUT_BEHIND:
                    finish(i - OUT_BEHIND)
                if i < TILES and not on_pool(i):
                    rounded(i)


def kernel(**inputs):
    import numpy as _np
    import concourse.bacc as _bacc
    from concourse import mybir as _mybir
    from concourse.bass_utils import run_bass_kernel_spmd as _run

    nc = _bacc.Bacc("TRN2", target_bir_lowering=False, num_devices=1)
    a = {k: _np.asarray(v) for k, v in inputs.items()}
    B, S, D = a["x"].shape
    arrays = {
        "in_x": _np.ascontiguousarray(a["x"].reshape(B * S, D)),
        "in_ids": _np.ascontiguousarray(a["itok_BxS_13_99985"].reshape(P, B * S // P)),
        "in_ctx_t": _np.ascontiguousarray(a["ctx_2048"].transpose(0, 2, 1)),
        "in_g_x": _np.ascontiguousarray(a["g_xattn"].reshape(1)),
        "in_g_f": _np.ascontiguousarray(a["g_ffn"].reshape(1)),
        "in_wf_t": _np.ascontiguousarray(a["L0_ffn_weight"].T),
    }
    args = [nc.dram_tensor(n, v.shape, _mybir.dt.from_np(v.dtype), kind="ExternalInput").ap()
            for n, v in arrays.items()]
    args.append(nc.dram_tensor("out_0", (B * S, D), _mybir.dt.float32, kind="ExternalOutput").ap())
    gated_experts_kernel(nc, *args)
    r = _run(nc, [arrays], core_ids=[0])
    return r.results[0]["out_0"].reshape(B, S, D)
```
